# Optimizing a Trainium2 kernel written in Bass

```python
import numpy as np
import jax
import jax.numpy as jnp

def _softmax(x, axis=-1):
    return jax.nn.softmax(x, axis=axis)

def _gelu(x):
    return jax.nn.gelu(x, approximate=True)

def _silu(x):
    return jax.nn.silu(x)

def _sigmoid(x):
    return jax.nn.sigmoid(x)

def _layernorm(x, axis=-1, eps=1e-05):
    m = jnp.mean(x, axis=axis, keepdims=True)
    v = jnp.var(x, axis=axis, keepdims=True)
    return (x - m) / jnp.sqrt(v + eps)

def _scatter_add(tgt, idx, src, axis=0):
    return tgt.at[idx].add(src)

def _segment_sum(src, seg, n):
    return jax.ops.segment_sum(src, seg, n)
kernel_name = 'mk_hybrid_d1_jaxref_r8_847b2b'

def setup_inputs(seed: int=0):
    np.random.seed(seed)
    _w = jnp.asarray

    def _L0_attn_a_setup():
        import jax, jax.numpy as jnp
        import numpy as np
        DIM = 256
        HEADS = 16
        HEAD_DIM = DIM // HEADS
        CHUNK = 128
        B, N = (4, 256)

        def _rmsnorm(x, w, eps):
            return x * jax.lax.rsqrt(jnp.mean(x * x, axis=-1, keepdims=True) + eps) * w

        def _weight_quant(w):
            scale = 1.0 / jnp.clip(jnp.mean(jnp.abs(w)), 1e-05, None)
            q = jnp.clip(jnp.round(w * scale), -1.0, 1.0) / scale
            return w + jax.lax.stop_gradient(q - w)

        def _forward(x, qkv_w, qkv_norm_w, proj_w, proj_norm_w, norm_w, s):
            Bb, Nn, C = x.shape
            H, D, T = (HEADS, HEAD_DIM, CHUNK)
            nc = Nn // T
            eps = jnp.finfo(x.dtype).eps
            scale = D ** (-0.5)
            h = _rmsnorm(x, qkv_norm_w, eps)
            qkv = h @ _weight_quant(qkv_w).T
            qkv = qkv.reshape(Bb, Nn, 3, H, D)
            q, k, v = (qkv[:, :, 0], qkv[:, :, 1], qkv[:, :, 2])

            def chunks(t):
                return t.reshape(Bb, nc, T, H, D).transpose(1, 0, 3, 2, 4)
            qc, kc, vc = (chunks(q), chunks(k), chunks(v))
            tt = jnp.arange(T, dtype=x.dtype)
            lam_t = jnp.exp(-s[:, None] * tt)
            lam_rev = jnp.exp(-s[:, None] * (T - tt))
            diff = tt[:, None] - tt[None, :]
            mask = jnp.where(diff >= 0, jnp.exp(-s[:, None, None] * diff), 0.0)
            lam_T = jnp.exp(-s * T)[:, None, None]

            def step(S, qkv_c):
                qi, ki, vi = qkv_c
                scores = jnp.einsum('bhtd,bhsd,hts->bhts', qi, ki, mask)
                intra = jnp.einsum('bhts,bhsd->bhtd', scores, vi)
                cross = jnp.einsum('bhtd,ht,bhde->bhte', qi, lam_t, S)
                o = scale * (intra + cross)
                kv = jnp.einsum('bhtd,ht,bhte->bhde', ki, lam_rev, vi)
                return (lam_T * S + kv, o)
            S0 = jnp.zeros((Bb, H, D, D), x.dtype)
            _, outs = jax.lax.scan(step, S0, (qc, kc, vc))
            out = outs.transpose(1, 0, 3, 2, 4).reshape(Bb, Nn, C)
            out = _rmsnorm(out, norm_w, 1e-06)
            out = _rmsnorm(out, proj_norm_w, eps) @ _weight_quant(proj_w).T
            return out
        key = jax.random.key(seed)
        ks = jax.random.split(key, 3)
        x = jax.random.normal(ks[0], (B, N, DIM), jnp.float32)
        bound = float(1.0 / np.sqrt(DIM))
        qkv_w = jax.random.uniform(ks[1], (3 * DIM, DIM), jnp.float32, -bound, bound)
        proj_w = jax.random.uniform(ks[2], (DIM, DIM), jnp.float32, -bound, bound)
        return {'x': x, 'qkv_w': qkv_w, 'qkv_norm_w': jnp.ones((DIM,), jnp.float32), 'proj_w': proj_w, 'proj_norm_w': jnp.ones((DIM,), jnp.float32), 'norm_w': jnp.ones((DIM,), jnp.float32), 's': jnp.full((HEADS,), 0.02, jnp.float32)}
    _L0_attn_a_in = _L0_attn_a_setup()

    def _L0_attn_b_setup():
        import jax, jax.numpy as jnp
        import numpy as np
        H = 16
        CHUNK = 64
        EPS = 1e-05

        def _forward(x, wq, wk, wv, wo, fq1_w, fq1_b, fq2_w, fq2_b, fk1_w, fk1_b, fk2_w, fk2_b, norm_w):
            B, L, D = x.shape
            dk = D // H

            def proj(w):
                return (x @ w.T).reshape(B, L, H, dk).transpose(0, 2, 1, 3)
            q, k, v = (proj(wq), proj(wk), proj(wv))
            q = (q @ fq1_w.T + fq1_b) * (q @ fq2_w.T + fq2_b)
            k = (k @ fk1_w.T + fk1_b) * (k @ fk2_w.T + fk2_b)
            scale = dk ** (-0.5)
            n = L // CHUNK
            qc = q.reshape(B, H, n, CHUNK, dk) * scale
            kc = k.reshape(B, H, n, CHUNK, dk)
            vc = v.reshape(B, H, n, CHUNK, dk)
            kv = jnp.einsum('bhncd,bhnce->bhnde', kc, vc)
            kv = jnp.cumsum(kv, axis=2)
            kv = jnp.concatenate([jnp.zeros_like(kv[:, :, :1]), kv[:, :, :-1]], axis=2)
            inter = jnp.einsum('bhncd,bhnde->bhnce', qc, kv)
            s = jnp.einsum('bhncd,bhnmd->bhncm', qc, kc)
            mask = jnp.tril(jnp.ones((CHUNK, CHUNK), bool))
            s = jnp.where(mask, s, 0.0)
            intra = jnp.einsum('bhncm,bhnmd->bhncd', s, vc)
            o = (inter + intra).reshape(B, H, L, dk)
            o = o * jax.lax.rsqrt(jnp.mean(o * o, axis=-1, keepdims=True) + EPS) * norm_w
            o = o.transpose(0, 2, 1, 3).reshape(B, L, D)
            return o @ wo.T
        key = jax.random.key(seed)
        ks = jax.random.split(key, 16)
        B, L, D = (2, 512, 256)
        dk = D // H
        g = 2 ** (-2.5)

        def xav(k, n):
            lim = g * np.sqrt(6.0 / (2 * n))
            return jax.random.uniform(k, (n, n), jnp.float32, -lim, lim)
        return {'x': jax.random.normal(ks[0], (B, L, D), jnp.float32), 'wq': xav(ks[1], D), 'wk': xav(ks[2], D), 'wv': xav(ks[3], D), 'wo': xav(ks[4], D), 'fq1_w': xav(ks[5], dk), 'fq1_b': jnp.zeros((dk,), jnp.float32), 'fq2_w': xav(ks[6], dk), 'fq2_b': jnp.zeros((dk,), jnp.float32), 'fk1_w': xav(ks[7], dk), 'fk1_b': jnp.zeros((dk,), jnp.float32), 'fk2_w': xav(ks[8], dk), 'fk2_b': jnp.zeros((dk,), jnp.float32), 'norm_w': jnp.ones((dk,), jnp.float32)}
    _L0_attn_b_in = _L0_attn_b_setup()

    def _L0_ffn_setup():
        import jax, jax.numpy as jnp
        import numpy as np
        B, S, H, E, D, K = (2, 256, 256, 8, 256, 2)
        key = jax.random.key(seed)
        ks = jax.random.split(key, 4)
        return {'x': jax.random.normal(ks[0], (B, S, H), jnp.float32), 'router_w': jax.random.normal(ks[1], (H, E), jnp.float32) / np.sqrt(H).astype(np.float32), 'router_b': jnp.zeros((E,), jnp.float32), 'expert_w': jax.random.normal(ks[2], (E, H, D), jnp.float32) / np.sqrt(H).astype(np.float32), 'expert_b': jnp.zeros((E, D), jnp.float32), 'out_w': jax.random.normal(ks[3], (D, D), jnp.float32) / np.sqrt(D).astype(np.float32), 'out_b': jnp.zeros((D,), jnp.float32)}
    _L0_ffn_in = _L0_ffn_setup()
    _d = {'L0_attn_a_x': _L0_attn_a_in['x'], 'L0_attn_a_qkv_w': _L0_attn_a_in['qkv_w'], 'L0_attn_a_qkv_norm_w': _L0_attn_a_in['qkv_norm_w'], 'L0_attn_a_proj_w': _L0_attn_a_in['proj_w'], 'L0_attn_a_proj_norm_w': _L0_attn_a_in['proj_norm_w'], 'L0_attn_a_norm_w': _L0_attn_a_in['norm_w'], 'L0_attn_a_s': _L0_attn_a_in['s'], 'L0_attn_b_wq': _L0_attn_b_in['wq'], 'L0_attn_b_wk': _L0_attn_b_in['wk'], 'L0_attn_b_wv': _L0_attn_b_in['wv'], 'L0_attn_b_wo': _L0_attn_b_in['wo'], 'L0_attn_b_fq1_w': _L0_attn_b_in['fq1_w'], 'L0_attn_b_fq1_b': _L0_attn_b_in['fq1_b'], 'L0_attn_b_fq2_w': _L0_attn_b_in['fq2_w'], 'L0_attn_b_fq2_b': _L0_attn_b_in['fq2_b'], 'L0_attn_b_fk1_w': _L0_attn_b_in['fk1_w'], 'L0_attn_b_fk1_b': _L0_attn_b_in['fk1_b'], 'L0_attn_b_fk2_w': _L0_attn_b_in['fk2_w'], 'L0_attn_b_fk2_b': _L0_attn_b_in['fk2_b'], 'L0_attn_b_norm_w': _L0_attn_b_in['norm_w'], 'L0_ffn_router_w': _L0_ffn_in['router_w'], 'L0_ffn_router_b': _L0_ffn_in['router_b'], 'L0_ffn_expert_w': _L0_ffn_in['expert_w'], 'L0_ffn_expert_b': _L0_ffn_in['expert_b'], 'L0_ffn_out_w': _L0_ffn_in['out_w'], 'L0_ffn_out_b': _L0_ffn_in['out_b']}
    _x0 = _d['L0_attn_a_x']
    _d['L0_attn_a_x'] = jax.random.normal(jax.random.fold_in(jax.random.key(seed), 1), (1, 1024, 256), dtype=_x0.dtype)
    del _x0
    return _d

def reference(L0_attn_a_x, L0_attn_a_qkv_w, L0_attn_a_qkv_norm_w, L0_attn_a_proj_w, L0_attn_a_proj_norm_w, L0_attn_a_norm_w, L0_attn_a_s, L0_attn_b_wq, L0_attn_b_wk, L0_attn_b_wv, L0_attn_b_wo, L0_attn_b_fq1_w, L0_attn_b_fq1_b, L0_attn_b_fq2_w, L0_attn_b_fq2_b, L0_attn_b_fk1_w, L0_attn_b_fk1_b, L0_attn_b_fk2_w, L0_attn_b_fk2_b, L0_attn_b_norm_w, L0_ffn_router_w, L0_ffn_router_b, L0_ffn_expert_w, L0_ffn_expert_b, L0_ffn_out_w, L0_ffn_out_b):

    def _L0_attn_a_ref(x, qkv_w, qkv_norm_w, proj_w, proj_norm_w, norm_w, s):
        import jax, jax.numpy as jnp
        import numpy as np
        DIM = 256
        HEADS = 16
        HEAD_DIM = DIM // HEADS
        CHUNK = 128
        B, N = (4, 256)

        def _rmsnorm(x, w, eps):
            return x * jax.lax.rsqrt(jnp.mean(x * x, axis=-1, keepdims=True) + eps) * w

        def _weight_quant(w):
            scale = 1.0 / jnp.clip(jnp.mean(jnp.abs(w)), 1e-05, None)
            q = jnp.clip(jnp.round(w * scale), -1.0, 1.0) / scale
            return w + jax.lax.stop_gradient(q - w)

        def _forward(x, qkv_w, qkv_norm_w, proj_w, proj_norm_w, norm_w, s):
            Bb, Nn, C = x.shape
            H, D, T = (HEADS, HEAD_DIM, CHUNK)
            nc = Nn // T
            eps = jnp.finfo(x.dtype).eps
            scale = D ** (-0.5)
            h = _rmsnorm(x, qkv_norm_w, eps)
            qkv = h @ _weight_quant(qkv_w).T
            qkv = qkv.reshape(Bb, Nn, 3, H, D)
            q, k, v = (qkv[:, :, 0], qkv[:, :, 1], qkv[:, :, 2])

            def chunks(t):
                return t.reshape(Bb, nc, T, H, D).transpose(1, 0, 3, 2, 4)
            qc, kc, vc = (chunks(q), chunks(k), chunks(v))
            tt = jnp.arange(T, dtype=x.dtype)
            lam_t = jnp.exp(-s[:, None] * tt)
            lam_rev = jnp.exp(-s[:, None] * (T - tt))
            diff = tt[:, None] - tt[None, :]
            mask = jnp.where(diff >= 0, jnp.exp(-s[:, None, None] * diff), 0.0)
            lam_T = jnp.exp(-s * T)[:, None, None]

            def step(S, qkv_c):
                qi, ki, vi = qkv_c
                scores = jnp.einsum('bhtd,bhsd,hts->bhts', qi, ki, mask)
                intra = jnp.einsum('bhts,bhsd->bhtd', scores, vi)
                cross = jnp.einsum('bhtd,ht,bhde->bhte', qi, lam_t, S)
                o = scale * (intra + cross)
                kv = jnp.einsum('bhtd,ht,bhte->bhde', ki, lam_rev, vi)
                return (lam_T * S + kv, o)
            S0 = jnp.zeros((Bb, H, D, D), x.dtype)
            _, outs = jax.lax.scan(step, S0, (qc, kc, vc))
            out = outs.transpose(1, 0, 3, 2, 4).reshape(Bb, Nn, C)
            out = _rmsnorm(out, norm_w, 1e-06)
            out = _rmsnorm(out, proj_norm_w, eps) @ _weight_quant(proj_w).T
            return out
        return _forward(x, qkv_w, qkv_norm_w, proj_w, proj_norm_w, norm_w, s)

    def _L0_attn_b_ref(x, wq, wk, wv, wo, fq1_w, fq1_b, fq2_w, fq2_b, fk1_w, fk1_b, fk2_w, fk2_b, norm_w):
        import jax, jax.numpy as jnp
        import numpy as np
        H = 16
        CHUNK = 64
        EPS = 1e-05

        def _forward(x, wq, wk, wv, wo, fq1_w, fq1_b, fq2_w, fq2_b, fk1_w, fk1_b, fk2_w, fk2_b, norm_w):
            B, L, D = x.shape
            dk = D // H

            def proj(w):
                return (x @ w.T).reshape(B, L, H, dk).transpose(0, 2, 1, 3)
            q, k, v = (proj(wq), proj(wk), proj(wv))
            q = (q @ fq1_w.T + fq1_b) * (q @ fq2_w.T + fq2_b)
            k = (k @ fk1_w.T + fk1_b) * (k @ fk2_w.T + fk2_b)
            scale = dk ** (-0.5)
            n = L // CHUNK
            qc = q.reshape(B, H, n, CHUNK, dk) * scale
            kc = k.reshape(B, H, n, CHUNK, dk)
            vc = v.reshape(B, H, n, CHUNK, dk)
            kv = jnp.einsum('bhncd,bhnce->bhnde', kc, vc)
            kv = jnp.cumsum(kv, axis=2)
            kv = jnp.concatenate([jnp.zeros_like(kv[:, :, :1]), kv[:, :, :-1]], axis=2)
            inter = jnp.einsum('bhncd,bhnde->bhnce', qc, kv)
            s = jnp.einsum('bhncd,bhnmd->bhncm', qc, kc)
            mask = jnp.tril(jnp.ones((CHUNK, CHUNK), bool))
            s = jnp.where(mask, s, 0.0)
            intra = jnp.einsum('bhncm,bhnmd->bhncd', s, vc)
            o = (inter + intra).reshape(B, H, L, dk)
            o = o * jax.lax.rsqrt(jnp.mean(o * o, axis=-1, keepdims=True) + EPS) * norm_w
            o = o.transpose(0, 2, 1, 3).reshape(B, L, D)
            return o @ wo.T
        return _forward(x, wq, wk, wv, wo, fq1_w, fq1_b, fq2_w, fq2_b, fk1_w, fk1_b, fk2_w, fk2_b, norm_w)

    def _L0_ffn_ref(x, router_w, router_b, expert_w, expert_b, out_w, out_b):
        import jax, jax.numpy as jnp
        import numpy as np
        B, S, H, E, D, K = (2, 256, 256, 8, 256, 2)
        num_experts = expert_w.shape[0]
        router_logits = jnp.einsum('bsh,he->bse', x, router_w) + router_b
        router_probs = jax.nn.softmax(router_logits, axis=-1)
        top_k_probs, top_k_indices = jax.lax.top_k(router_probs, K)
        top_k_probs = top_k_probs / jnp.sum(top_k_probs, axis=-1, keepdims=True)
        onehot = jax.nn.one_hot(top_k_indices, num_experts, dtype=x.dtype)
        gates = jnp.einsum('bsk,bske->bse', top_k_probs, onehot)
        expert_out = jax.nn.gelu(jnp.einsum('bsh,ehd->ebsd', x, expert_w) + expert_b[:, None, None, :])
        combined = jnp.einsum('bse,ebsd->bsd', gates, expert_out)
        return jnp.einsum('bsd,df->bsf', combined, out_w) + out_b
    x = L0_attn_a_x
    x = x + _L0_attn_a_ref(_layernorm(x, axis=-1), L0_attn_a_qkv_w, L0_attn_a_qkv_norm_w, L0_attn_a_proj_w, L0_attn_a_proj_norm_w, L0_attn_a_norm_w, L0_attn_a_s)
    x = x + _L0_ffn_ref(_layernorm(x, axis=-1), L0_ffn_router_w, L0_ffn_router_b, L0_ffn_expert_w, L0_ffn_expert_b, L0_ffn_out_w, L0_ffn_out_b)
    x = x + _L0_attn_b_ref(_layernorm(x, axis=-1), L0_attn_b_wq, L0_attn_b_wk, L0_attn_b_wv, L0_attn_b_wo, L0_attn_b_fq1_w, L0_attn_b_fq1_b, L0_attn_b_fq2_w, L0_attn_b_fq2_b, L0_attn_b_fk1_w, L0_attn_b_fk1_b, L0_attn_b_fk2_w, L0_attn_b_fk2_b, L0_attn_b_norm_w)
    x = x + _L0_ffn_ref(_layernorm(x, axis=-1), L0_ffn_router_w, L0_ffn_router_b, L0_ffn_expert_w, L0_ffn_expert_b, L0_ffn_out_w, L0_ffn_out_b)
    return x

_drawn_inputs = setup_inputs


def setup_inputs(seed=0):
    import zlib

    import numpy as np

    out = dict(_drawn_inputs(seed))
    spreads = {'L0_attn_a_qkv_norm_w': (1.0, 0.2),
     'L0_attn_a_proj_norm_w': (1.0, 0.2),
     'L0_attn_a_norm_w': (1.0, 0.2),
     'L0_attn_a_s': (0.019999999552965164, 0.2),
     'L0_attn_b_fq1_b': (0.0, 0.1),
     'L0_attn_b_fq2_b': (0.0, 0.1),
     'L0_attn_b_fk1_b': (0.0, 0.1),
     'L0_attn_b_fk2_b': (0.0, 0.1),
     'L0_attn_b_norm_w': (1.0, 0.594),
     'L0_ffn_router_b': (0.0, 0.1),
     'L0_ffn_expert_b': (0.0, 0.1),
     'L0_ffn_out_b': (0.0, 0.1)}
    factors = {'L0_attn_b_fk2_w': 2.975}
    for name, (base, spread) in spreads.items():
        noise = np.random.default_rng([zlib.crc32(name.encode()), seed]).standard_normal(out[name].shape)
        drawn = base * np.exp(spread * noise) if base else spread * noise
        out[name] = jnp.asarray(drawn.astype(out[name].dtype))
    for name, factor in factors.items():
        out[name] = (out[name] * factor).astype(out[name].dtype)
    return out
```

```python
from contextlib import ExitStack

import numpy as np

import concourse.bass as bass
from concourse import mybir

F32 = mybir.dt.float32
F32R = mybir.dt.float32r
U32 = mybir.dt.uint32
ALU = mybir.AluOpType
ACT = mybir.ActivationFunctionType
AX = mybir.AxisListType

P = 128
T = 1024
D = 256
KH = D // P
HEADS = 16
DH = D // HEADS
NT = T // P
E = 8
GROUPS = E * D // 512
SLOTS = HEADS
EPS32 = float(np.finfo(np.float32).eps)
LN_EPS = 1e-5
NORM_EPS = 1e-6
HEAD_EPS = 1e-5
QK_SCALE = DH ** -0.5

C_ID, C_ONE, C_CAUSAL, C_DIFF, C_BLOCK, C_TT, C_PAIR, C_IOTA, C_EVEN, C_ODD, C_SECOND, C_REV, C_END = (
    0, 128, 256, 384, 512, 640, 768, 896, 904, 905, 906, 907, 908)
S_DECAY, S_HNORM, S_ROUTER, S_S, S_END = 0, 2, 3, 19, 35
R_QKVN, R_NORM, R_PROJN, R_B1, R_B2, R_OUTB, R_RB, R_END = (
    0, 256, 512, 768, 1280, 1792, 2048, 2056)


def head_of(j, i):
    return 8 * (i // 2) + 2 * j + i % 2


def build(nc, x, cst, small, rows, wqkv, wproj, bdiag, wq, wk, wv, wo, wexp, bexp, wout, out):
    with ExitStack() as ctx:
        def sb(name, shape, dt=F32):
            return ctx.enter_context(nc.sbuf_tensor(name, shape, dt))

        def sem(name):
            return ctx.enter_context(nc.semaphore(name))

        def psum(name, shape):
            return ctx.enter_context(nc.psum_tensor(name, shape, F32))

        S = psum("S", [P, 4 * 512])
        TA = psum("TA", [P, 512])
        TF = psum("TF", [P, 512])
        EX = psum("EX", [P, 2, 512])

        xs = sb("xs", [P, NT, D])
        c = sb("c", [P, C_END])
        sm = sb("sm", [P, S_END])
        rw = sb("rw", [P, R_END])
        wqkv_f = sb("wqkv_f", [P, KH, 3 * D])
        wproj_f = sb("wproj_f", [P, KH, D])
        wqkv_t = sb("wqkv_t", [P, KH, 3 * D], F32R)
        wproj_t = sb("wproj_t", [P, KH, D], F32R)
        bd = sb("bd", [P, 4, P])
        norm2 = sb("norm2", [P, D])
        wq_n = sb("wq_n", [P, KH, D])
        wk_n = sb("wk_n", [P, KH, D])
        wv_f = sb("wv_f", [P, KH, D])
        wo_f = sb("wo_f", [P, KH, D])
        wo_s = sb("wo_s", [P, KH, D])
        wb_hi = sb("wb_hi", [P, KH, 5 * D], F32R)
        wb_lo = sb("wb_lo", [P, KH, 5 * D], F32R)
        wo_hi = sb("wo_hi", [P, KH, D], F32R)
        wo_lo = sb("wo_lo", [P, KH, D], F32R)
        we_f = sb("we_f", [P, KH, E * D])
        xf = we_f[:].rearrange("p k n -> p (k n)").rearrange("p (t d) -> p t d", d=D)
        we_hi = sb("we_hi", [P, KH, E * D], F32R)
        we_lo = sb("we_lo", [P, KH, E * D], F32R)
        be_f = sb("be_f", [2, E * D])
        be = sb("be", [P, E * D], F32R)
        pair = sb("pair", [P, P], F32R)
        wout_f = sb("wout_f", [P, KH, D])
        wout_hi = sb("wout_hi", [P, KH, D], F32R)
        wout_lo = sb("wout_lo", [P, KH, D], F32R)
        wr_hi = sb("wr_hi", [P, KH, E], F32R)
        wr_lo = sb("wr_lo", [P, KH, E], F32R)
        absum = sb("absum", [P, 2])
        wmean = sb("wmean", [P, 2])
        wscale = sb("wscale", [P, 2])
        neg_s = sb("neg_s", [P, HEADS])
        neg_sf = sb("neg_sf", [P, KH])
        mhalf = sb("mhalf", [P, HEADS])
        decay = sb("decay", [P, SLOTS, P])
        lam_q = sb("lam_q", [P, KH, P])
        lam_k = sb("lam_k", [P, HEADS])
        lam_p = sb("lam_p", [P, KH])

        st_a = sb("st_a", [P, 6])
        mv_a = sb("mv_a", [P, 2])
        var_a = sb("var_a", [P, 1])
        rs_a = sb("rs_a", [P, 1])
        hn = sb("hn", [P, D])
        h_hi = sb("h_hi", [P, D], F32R)
        h_lo = sb("h_lo", [P, D], F32R)
        f1 = sb("f1", [P, 512])
        f2 = sb("f2", [P, 512])
        qk = sb("qk", [P, 512])
        v = sb("v", [P, D])
        qT = sb("qT", [P, KH, P])
        qTl = sb("qTl", [P, KH, P])
        kT = sb("kT", [P, 2, KH, P])
        o_sb = sb("o_sb", [P, D])
        kl = sb("kl", [P, D])
        pr = sb("pr", [P, SLOTS, P])
        state_a = sb("state_a", [P, KH, P])
        state_b = sb("state_b", [P, KH, P])
        sbd_a = sb("sbd_a", [P, KH, P])
        sbd_b = sb("sbd_b", [P, KH, P])
        z1 = sb("z1", [P, D])
        z2 = sb("z2", [P, D])
        sq = sb("sq", [P, D])
        sq2 = sb("sq2", [P, D])
        sums = sb("sums", [P, 2])
        u1 = sb("u1", [P, 1])
        u2 = sb("u2", [P, HEADS])
        r2 = sb("r2", [P, HEADS])
        r2m = sb("r2m", [P, 1])
        z_hi = sb("z_hi", [P, D], F32R)
        z_lo = sb("z_lo", [P, D], F32R)
        xc = sb("xc", [P, D])

        st_f = sb("st_f", [P, 6])
        mv_f = sb("mv_f", [P, 2])
        var_f = sb("var_f", [P, 1])
        rs_f = sb("rs_f", [P, 1])
        xn = sb("xn", [P, D])
        xr = sb("xr", [P, D])
        x_hi = sb("x_hi", [P, D], F32R)
        x_lo = sb("x_lo", [P, D], F32R)
        lg = sb("lg", [P, E])
        m8 = sb("m8", [P, E])
        ix = sb("ix", [P, E], U32)
        ixf = sb("ixf", [P, 2])
        dl = sb("dl", [P, 1])
        th = sb("th", [P, 1])
        g12 = sb("g12", [P, 2])
        oh = sb("oh", [P, 2, E])
        gates = sb("gates", [P, E])
        hb = sb("hb", [P, GROUPS, 512])
        acc = sb("acc", [P, 2, D])
        tern_tmp = pr[:].rearrange("p s t -> p (s t)")[:, 0:KH * 3 * D]
        tern_lt = hb[:].rearrange("p g n -> p (g n)")[:, 0:KH * 3 * D]
        tern2 = wo_s[:].rearrange("p k n -> p (k n)")
        a_hi = sb("a_hi", [P, D], F32R)
        a_lo = sb("a_lo", [P, D], F32R)

        ld_c, ld_sm, ld_rows, ld_x0, ld_x = sem("ld_c"), sem("ld_sm"), sem("ld_rows"), sem("ld_x0"), sem("ld_x")
        ld_norms = sem("ld_norms")
        ld_wqkv, ld_wproj, ld_b, ld_e, ld_be, ld_wout = (
            sem("ld_wqkv"), sem("ld_wproj"), sem("ld_b"), sem("ld_e"), sem("ld_be"), sem("ld_wout"))
        s_abs, s_sum, s_mean, s_scaled, s_lt, s_tern = (
            sem("s_abs"), sem("s_sum"), sem("s_mean"), sem("s_scaled"), sem("s_lt"), sem("s_tern"))
        s_neg, s_exp, s_decay, s_fill = sem("s_neg"), sem("s_exp"), sem("s_decay"), sem("s_fill")
        s_fold, s_bhi, s_blo, s_wos = sem("s_fold"), sem("s_bhi"), sem("s_blo"), sem("s_wos")
        s_ehi, s_elo, s_be = sem("s_ehi"), sem("s_elo"), sem("s_be")
        at_st, at_mv, at_u, at_rs, at_h, at_hT, at_hi, at_lo = (
            sem("at_st"), sem("at_mv"), sem("at_u"), sem("at_rs"), sem("at_h"), sem("at_hT"), sem("at_hi"), sem("at_lo"))
        at_proj, at_projv, at_f, at_qk, at_v, at_turned, at_qT, at_kT, at_ql, at_kl = (
            sem("at_proj"), sem("at_projv"), sem("at_f"), sem("at_qk"), sem("at_v"), sem("at_turned"), sem("at_qT"), sem("at_kT"),
            sem("at_ql"), sem("at_kl"))
        at_sc, at_p, at_kv, at_ocopy, at_o, at_state, at_sbd = sem("at_sc"), sem("at_p"), sem("at_kv"), sem("at_ocopy"), sem("at_o"), sem("at_state"), sem("at_sbd")
        at_sq, at_z1, at_u1, at_u2, at_r2, at_z2, at_zT, at_zhi, at_zlo, at_y, at_x = (
            sem("at_sq"), sem("at_z1"), sem("at_u1"), sem("at_u2"), sem("at_r2"), sem("at_z2"), sem("at_zT"),
            sem("at_zhi"), sem("at_zlo"), sem("at_y"), sem("at_x"))
        f_st, f_mv, f_u, f_rs, f_xn, f_xr, f_T, f_hi, f_lo, f_lg = (
            sem("f_st"), sem("f_mv"), sem("f_u"), sem("f_rs"), sem("f_xn"), sem("f_xr"), sem("f_T"), sem("f_hi"),
            sem("f_lo"), sem("f_lg"))
        f_g, f_d, f_th, f_ex, f_gelu, f_acc, f_aT, f_ahi, f_alo, f_y, f_x = (
            sem("f_g"), sem("f_d"), sem("f_th"), sem("f_ex"), sem("f_gelu"), sem("f_acc"), sem("f_aT"), sem("f_ahi"),
            sem("f_alo"), sem("f_y"), sem("f_x"))
        passed, s_pow, s_pow2, s_sq2 = sem("passed"), sem("s_pow"), sem("s_pow2"), sem("s_sq2")
        st_out, s_norm2 = sem("st_out"), sem("s_norm2")

        ident = c[:, C_ID:C_ID + P]
        causal = c[:, C_CAUSAL:C_CAUSAL + P]
        out_t = out[0].rearrange("(t p) d -> t p d", p=P)
        x_t = x[0].rearrange("(t p) d -> p t d", p=P)

        G_STEPS = 8

        def since(eng, s, n):
            if not isinstance(n, int) or n > 0:
                eng.wait_ge(s, n)

        def steps(eng, step, between):
            step(0, "a", None, "a", False, False)
            between()
            step(1, "a", "a", "a", True, False)
            with eng.Fori(2, NT - 1) as n:
                step(n, "a", "a", "a", True, True)
            step(NT - 1, "a", "a", "b", True, True)
            step(NT, "b", "a", "b", True, True)
            with eng.Fori(NT + 1, 2 * NT - 1) as n:
                step(n, "b", "b", "b", True, True)
            step(2 * NT - 1, "b", "b", None, True, True)
            step(2 * NT, None, "b", None, True, True)
            step(2 * NT + 1, None, None, None, False, True)

        block = ctx.enter_context(nc.Block())

        @block.sync
        def _(sp):
            sp.dma_start(sm[:], small).then_inc(ld_sm, 16)
            sp.dma_start(c[:], cst).then_inc(ld_c, 16)
            sp.dma_start(wqkv_f[:], wqkv).then_inc(ld_wqkv, 16)
            sp.dma_start(xs[:, 0, :], x_t[:, 0, :]).then_inc(ld_x0, 16)
            sp.dma_start(rw[:, 0:R_B1], rows[:, 0:R_B1].to_broadcast([P, R_B1])).then_inc(ld_norms, 16)
            sp.dma_start(wproj_f[:], wproj).then_inc(ld_wproj, 16)
            sp.dma_start(xs[:, 1:NT, :], x_t[:, 1:NT, :]).then_inc(ld_x, 16)
            sp.dma_start(we_f[:], wexp).then_inc(ld_e, 16)
            sp.dma_start(be_f[:], bexp).then_inc(ld_be, 16)
            sp.dma_start(wout_f[:], wout).then_inc(ld_wout, 16)
            sp.dma_start(rw[:, R_B1:R_END], rows[:, R_B1:R_END].to_broadcast([P, R_END - R_B1])).then_inc(ld_rows, 16)
            for to, w in ((bd, bdiag), (wq_n, wq), (wk_n, wk), (wv_f, wv), (wo_f, wo)):
                sp.dma_start(to[:], w).then_inc(ld_b, 16)
            with sp.Fori(0, NT) as t:
                to = out_t[bass.ds(t, 1)]
                tile = xf[:, bass.ds(t + NT, 1), :]
                sp.wait_ge(f_x, t + NT + 1)
                sp.dma_start(to, tile).then_inc(st_out, 16)
            sp.wait_ge(st_out, 16 * NT)

        @block.gpsimd
        def _(pool):
            pool.memset(mhalf[:], -0.5)
            pool.memset(state_a[:], 0.0)
            pool.memset(state_b[:], 0.0)
            pool.memset(sbd_a[:], 0.0)
            pool.memset(sbd_b[:], 0.0).then_inc(at_sbd, 1)
            pool.memset(be[:].bitcast(F32), 0.0).then_inc(s_fill, 1)
            pool.wait_ge(s_fill, 1)
            def start(kind, n):
                since(pool, at_v, n)
                since(pool, at_u, n + 1)
                if kind == "a":
                    pool.tensor_tensor(rs_a[:], var_a[:], mhalf[:, 0:1], ALU.pow).then_inc(s_pow, 1)
                    pool.wait_ge(s_pow, n + 1)
                    pool.tensor_tensor(rs_a[:], rs_a[:], wmean[:, 0:1], ALU.mult).then_inc(at_rs, 1)
                else:
                    pool.tensor_tensor(rs_a[:], var_a[:], mhalf[:, 0:1], ALU.pow).then_inc(at_rs, 1)

            def decayed_k(n):
                since(pool, at_qk, 2 * n + 2)
                pool.tensor_tensor(kl[:].rearrange("p (h d) -> p h d", d=DH),
                                   qk[:, D:2 * D].rearrange("p (h d) -> p h d", d=DH),
                                   lam_k[:].unsqueeze(2).to_broadcast([P, HEADS, DH]), ALU.mult).then_inc(at_kl, 1)

            def decayed_q(n):
                since(pool, at_qT, n + 1)
                pool.tensor_tensor(qTl[:], qT[:], lam_q[:], ALU.mult).then_inc(at_ql, 1)

            def products(n):
                since(pool, at_f, n - NT + 1)
                pool.tensor_tensor(qk[:, 0:D], f1[:, 0:D], f2[:, 0:D], ALU.mult).then_inc(at_qk, 1)

            def norms(kind, n):
                if kind == "a":
                    since(pool, at_u2, n + 1)
                    pool.tensor_tensor(r2[:, 0:1], u2[:, 0:1], mhalf[:, 0:1], ALU.pow).then_inc(s_pow2, 1)
                    pool.wait_ge(s_pow2, n + 1)
                    pool.tensor_tensor(r2m[:], r2[:, 0:1], wmean[:, 1:2], ALU.mult).then_inc(at_r2, 1)
                else:
                    since(pool, at_u2, n + 1)
                    pool.tensor_tensor(r2[:], u2[:], mhalf[:], ALU.pow).then_inc(at_r2, 1)

            def own_heads(kind, n):
                since(pool, at_state, n + 1)
                state, sbd = (state_a, sbd_a) if kind == "a" else (state_b, sbd_b)
                pool.tensor_tensor(sbd[:], state[:], c[:, C_BLOCK:C_BLOCK + P].unsqueeze(1).to_broadcast([P, KH, P]),
                                   ALU.mult).then_inc(at_sbd, 1)

            def root_x(n):
                since(pool, f_u, n + 1)
                pool.tensor_tensor(rs_f[:], var_f[:], mhalf[:, 0:1], ALU.pow).then_inc(f_rs, 1)

            def biased_x(u):
                since(pool, f_x, u)
                pool.tensor_tensor(xr[:], xc[:], rw[:, R_OUTB:R_OUTB + D], ALU.add).then_inc(f_xr, 1)

            def step(n, kind, last, front, mix, tail):
                if front:
                    start(front, n + 1)
                if last:
                    root_x(n - 1)
                if kind:
                    own_heads(kind, n)
                if front == "a":
                    decayed_k(n + 1)
                if front == "b":
                    products(n + 1)
                if kind:
                    norms(kind, n)
                if front == "a":
                    decayed_q(n + 1)
                if mix:
                    biased_x(n - 1)

            def between():
                pool.wait_ge(ld_rows, 16)
                pool.wait_ge(s_ehi, 1)
                pool.tensor_tensor(we_lo[:, 1, :], we_f[:, 1, :], we_hi[:, 1, :].bitcast(F32),
                                   ALU.subtract).then_inc(s_elo, 1)

            pool.wait_ge(ld_norms, 16)
            pool.wait_ge(ld_c, 16)
            pool.wait_ge(s_exp, 1)
            pool.wait_ge(s_mean, 1)
            pool.tensor_tensor(norm2[:], rw[:, R_NORM:R_NORM + D], rw[:, R_PROJN:R_PROJN + D],
                               ALU.mult).then_inc(s_norm2, 1)
            start("a", 0)
            decayed_k(0)
            decayed_q(0)
            pool.wait_ge(s_mean, 2)
            steps(pool, step, between)

        @block.scalar
        def _(act):
            act.wait_ge(ld_c, 16)
            act.wait_ge(s_neg, 2)
            for j in range(4):
                for i in range(4):
                    h = head_of(j, i)
                    act.activation(decay[:, 4 * j + i, :], c[:, C_DIFF:C_DIFF + P], ACT.Exp,
                                   scale=neg_s[:, h:h + 1])
            for k in range(KH):
                act.activation(lam_q[:, k, :], c[:, C_TT:C_TT + P], ACT.Exp, scale=neg_sf[:, k:k + 1])
            act.activation(lam_p[:], neg_sf[:], ACT.Exp, scale=float(P))
            act.activation(lam_k[:], neg_s[:], ACT.Exp, scale=c[:, C_REV:C_REV + 1]).then_inc(s_exp, 1)
            act.wait_ge(s_mean, 1)
            act.preload_act_table(ACT.Gelu_apprx_tanh)
            act.activation(tern_tmp, wqkv_f[:].rearrange("p k n -> p (k n)"), ACT.Copy,
                           scale=wscale[:, 0:1]).then_inc(s_scaled, 1)

            def second_ternary():
                act.wait_ge(s_mean, 2)
                act.activation(tern2, wproj_f[:].rearrange("p k n -> p (k n)"), ACT.Copy,
                               scale=wscale[:, 1:2]).then_inc(s_scaled, 1)

            def hi_h(n):
                since(act, at_hT, n + 1)
                act.activation(h_hi[:], S[:, 0:D], ACT.Copy).then_inc(at_hi, 1)

            def hi_x(u):
                since(act, f_T, u + 1)
                act.activation(x_hi[:], TF[:, D:2 * D], ACT.Copy).then_inc(f_hi, 1)

            def evac_qk(kind, n):
                since(act, at_rs, n + 1)
                if kind == "a":
                    since(act, at_proj, n + 1)
                    act.activation(qk[:, 0:D], S[:, 0:D], ACT.Copy, scale=rs_a[:, 0:1]).then_inc(at_qk, 1)
                    act.activation(qk[:, D:2 * D], S[:, D:2 * D], ACT.Copy, scale=rs_a[:, 0:1]).then_inc(at_qk, 1)

            def evac_v(kind, n):
                v0 = 2 * D if kind == "a" else 4 * D
                since(act, at_projv, n + 1)
                act.activation(v[:], S[:, v0:v0 + D], ACT.Copy, scale=rs_a[:, 0:1]).then_inc(at_v, 1)

            def evac_qT(n):
                since(act, at_turned, 2 * n + 1)
                act.activation(qT[:], S[:, 1536:1536 + D].rearrange("p (k t) -> p k t", k=KH), ACT.Copy).then_inc(at_qT, 1)

            def squares(kind, n):
                since(act, at_o, n + 1)
                if kind == "a":
                    act.activation(o_sb[:], TA[:, 0:D], ACT.Copy).then_inc(at_ocopy, 1)
                    since(act, at_ocopy, n + 1)
                    act.activation(sq[:], o_sb[:], ACT.Square, accum_out=sums[:, 0:1]).then_inc(at_sq, 1)
                else:
                    act.activation(sq[:], TA[:, 0:D], ACT.Square).then_inc(at_sq, 1)

            def squares_z(n):
                    since(act, at_z1, n + 1)
                    act.activation(sq2[:], z1[:], ACT.Square, accum_out=sums[:, 1:2]).then_inc(s_sq2, 1)

            def hi_z(n):
                since(act, at_zT, n + 1)
                act.activation(z_hi[:], TA[:, 0:D], ACT.Copy).then_inc(at_zhi, 1)

            def tanh(u):
                since(act, f_d, u + 1)
                act.activation(th[:], dl[:], ACT.Tanh, scale=0.5).then_inc(f_th, 1)

            def gelu(u, g):
                since(act, f_ex, GROUPS * u + g + 1)
                act.activation(hb[:, g, :], EX[:, g % 2, :], ACT.Gelu_apprx_tanh).then_inc(f_gelu, 1)

            def hi_a(u):
                since(act, f_aT, u + 1)
                act.activation(a_hi[:], TF[:, 0:D], ACT.Copy).then_inc(f_ahi, 1)

            def step(n, kind, last, front, mix, tail):
                if last:
                    hi_z(n - 1)
                if tail:
                    gelu(n - 2, 2)
                if mix:
                    hi_x(n - 1)
                if front:
                    hi_h(n + 1)
                if tail:
                    gelu(n - 2, 3)
                if front:
                    evac_qk(front, n + 1)
                if mix:
                    tanh(n - 1)
                    gelu(n - 1, 0)
                if tail:
                    hi_a(n - 2)
                if kind:
                    squares(kind, n)
                if front:
                    evac_qT(n + 1)
                    evac_v(front, n + 1)
                if kind == "a":
                    squares_z(n)
                if mix:
                    gelu(n - 1, 1)

            def between():
                act.activation(wr_hi[:], sm[:, S_ROUTER:S_ROUTER + KH * E].rearrange("p (k e) -> p k e", k=KH), ACT.Copy)
                act.activation(pair[:], c[:, C_PAIR:C_PAIR + P], ACT.Copy)
                act.wait_ge(ld_be, 16)
                act.wait_ge(s_fill, 1)
                act.activation(be[0:2, :], be_f[:], ACT.Copy).then_inc(s_be, 1)
                act.wait_ge(ld_wout, 16)
                act.activation(wout_hi[:], wout_f[:], ACT.Copy)
                act.wait_ge(ld_b, 16 * 5)
                act.activation(wb_hi[:, :, 4 * D:5 * D], wv_f[:], ACT.Copy)
                act.wait_ge(s_fold, 1)
                act.activation(wb_hi[:, :, 0:4 * D], S[:].rearrange("p (k n) -> p k n", k=KH), ACT.Copy)
                act.wait_ge(s_wos, 1)
                act.activation(wo_hi[:], wo_s[:], ACT.Copy).then_inc(s_bhi, 1)

            act.wait_ge(ld_wproj, 16)
            second_ternary()
            hi_h(0)
            evac_qk("a", 0)
            evac_v("a", 0)
            evac_qT(0)
            act.wait_ge(ld_e, 16)
            act.activation(we_hi[:], we_f[:], ACT.Copy).then_inc(s_ehi, 1)
            steps(act, step, between)

        @block.tensor
        def _(pe):
            pe.wait_ge(ld_c, 16)
            for m in range(2):
                pe.wait_ge(s_abs, m + 1)
                pe.matmul((TA, TF)[m][:, 0:1], c[:, C_ONE:C_ONE + P], absum[:, m:m + 1], start=True, stop=True).then_inc(s_sum, 1)
            def turn_h(n):
                since(pe, at_h, n + 1)
                since(pe, at_p, 2 * n - 1)
                for k in range(KH):
                    last = pe.transpose(S[:, P * k:P * k + P], hn[:, P * k:P * k + P], ident)
                last.then_inc(at_hT, 1)

            def project(kind, n, part):
                if part == "qk":
                    since(pe, at_hi, n + 1)
                    since(pe, at_lo, n + 1)
                w_hi, w_lo, width = (wqkv_t, None, 3 * D) if kind == "a" else (wb_hi, wb_lo, 5 * D)
                passes = [(h_hi, w_hi), (h_lo, w_hi)] + ([(h_hi, w_lo)] if w_lo is not None else [])
                n0, n1, done = (0, width - D, at_proj) if part == "qk" else (width - D, width, at_projv)
                for k in range(KH):
                    for i, (h, w) in enumerate(passes):
                        for c0 in range(n0, n1, 512):
                            c1 = min(c0 + 512, n1)
                            last = pe.matmul(S[:, c0:c1], h[:, P * k:P * k + P], w[:, k, c0:c1],
                                             start=(k == 0 and i == 0), stop=(k == KH - 1 and i == len(passes) - 1))
                last.then_inc(done, 1)

            def turn_qk(n):
                since(pe, at_qk, 2 * n + 2)
                for base, m in ((1536, 0), (0, 1)):
                    for f in range(KH):
                        last = pe.transpose(S[:, base + P * f:base + P * f + P],
                                            qk[:, D * m + P * f:D * m + P * f + P], ident)
                    last.then_inc(at_turned, 1)

            def scores(n, half, u=None, last_z=False):
                if half == 0:
                    since(pe, at_qT, n + 1)
                    since(pe, at_kT, n + 1)
                    since(pe, at_v, n + 1)
                for m in range(8):
                    i, j = m // 2, 2 * half + m % 2
                    rows_j = slice(32 * j, 32 * j + 32)
                    last = pe.matmul(S[:, 512 * j + P * i:512 * j + P * i + P], kT[rows_j, i % 2, i // 2, :],
                                     qT[rows_j, i // 2, :], start=True, stop=True)
                    if m == 7:
                        last.then_inc(at_sc, 1)
                    elif u is not None:
                        expert(u, 2 + half, m)
                    if m == 3 and last_z:
                        turn_z(n - 1)

            def state_products(kind, n):
                since(pe, at_x, n)
                since(pe, at_sbd, n + 1)
                q, sbd = (qT, sbd_b) if kind == "b" else (qTl, sbd_a)
                if kind == "a":
                    since(pe, at_ql, n + 1)
                    since(pe, at_kl, n + 1)
                for f in range(KH):
                    pe.matmul(TA[:, P * f:P * f + P], q[:, f, :], sbd[:, f, :], start=(f == 0), stop=False,
                              skip_group_check=True)
                for f in range(KH):
                    lhs = qk[:, D + P * f:D + P * f + P] if kind == "b" else kl[:, P * f:P * f + P]
                    last = pe.matmul(TA[:, D + P * f:D + P * f + P], lhs, v[:, P * f:P * f + P], start=False, stop=True,
                                     skip_group_check=True)
                last.then_inc(at_kv, 1)

            def heads(n, half, u=None):
                if half == 0:
                    since(pe, at_state, n + 1)
                since(pe, at_p, 2 * n + 1 + half)
                for m in range(8):
                    j, i = 2 * half + m // 4, m % 4
                    h = head_of(j, i)
                    last = pe.matmul(TA[:, DH * h:DH * h + DH], pr[:, 4 * j + i, :], v[:, DH * h:DH * h + DH],
                                     start=False, stop=True, skip_group_check=True)
                    if m < 7 and u is not None:
                        expert(u, half, m)
                if half == 1:
                    last.then_inc(at_o, 1)

            def turn_z(n):
                since(pe, at_z2, n + 1)
                for k in range(KH):
                    last = pe.transpose(TA[:, P * k:P * k + P], z2[:, P * k:P * k + P], ident)
                last.then_inc(at_zT, 1)

            def project_out(kind, n):
                since(pe, at_zhi, n + 1)
                since(pe, at_zlo, n + 1)
                w_hi, w_lo = (wproj_t, None) if kind == "a" else (wo_hi, wo_lo)
                passes = [(z_hi, w_hi), (z_lo, w_hi)] + ([(z_hi, w_lo)] if w_lo is not None else [])
                for k in range(KH):
                    for i, (z, w) in enumerate(passes):
                        last = pe.matmul(TA[:, D:2 * D], z[:, P * k:P * k + P], w[:, k, :],
                                         start=(k == 0 and i == 0), stop=(k == KH - 1 and i == len(passes) - 1))
                last.then_inc(at_y, 1)

            def turn_x(u):
                since(pe, f_xn, u + 1)
                for k in range(KH):
                    last = pe.transpose(TF[:, D + P * k:D + P * k + P], xn[:, P * k:P * k + P], ident)
                last.then_inc(f_T, 1)

            def router(u):
                since(pe, f_hi, u + 1)
                since(pe, f_lo, u + 1)
                for k in range(KH):
                    for i, (h, w) in enumerate(((x_hi, wr_hi), (x_hi, wr_lo), (x_lo, wr_hi))):
                        last = pe.matmul(TF[:, D:D + E], h[:, P * k:P * k + P], w[:, k, :],
                                         start=(k == 0 and i == 0), stop=(k == KH - 1 and i == 2))
                last.then_inc(f_lg, 1)

            def expert(u, g, m):
                cols = slice(512 * g, 512 * g + 512)
                if m == 0:
                    since(pe, f_gelu, GROUPS * u + g - 1)
                    pe.matmul(EX[:, g % 2, :], pair[:], be[:, cols], start=True, stop=False)
                else:
                    k, i = (m - 1) // 3, (m - 1) % 3
                    h, w = ((x_hi, we_hi), (x_hi, we_lo), (x_lo, we_hi))[i]
                    last = pe.matmul(EX[:, g % 2, :], h[:, P * k:P * k + P], w[:, k, cols],
                                     start=False, stop=(m == 6))
                    if m == 6:
                        last.then_inc(f_ex, 1)

            def experts(u, g):
                for m in range(7):
                    expert(u, g, m)

            def turn_a(u, last_tile):
                since(pe, f_acc, E * u + E)
                if not last_tile:
                    since(pe, f_g, G_STEPS * (u + 1) + 1)
                for k in range(KH):
                    last = pe.transpose(TF[:, P * k:P * k + P], acc[:, 1, P * k:P * k + P], ident)
                last.then_inc(f_aT, 1)

            def mix_out(u):
                since(pe, f_ahi, u + 1)
                since(pe, f_alo, u + 1)
                for k in range(KH):
                    for i, (h, w) in enumerate(((a_hi, wout_hi), (a_hi, wout_lo), (a_lo, wout_hi))):
                        last = pe.matmul(TF[:, 0:D], h[:, P * k:P * k + P], w[:, k, :],
                                         start=(k == 0 and i == 0), stop=(k == KH - 1 and i == 2))
                last.then_inc(f_y, 1)

            def step(n, kind, last, front, mix, tail):
                if kind:
                    scores(n, 0, n - 2 if tail else None, last is not None)
                elif tail:
                    if last:
                        turn_z(n - 1)
                    experts(n - 2, 2)
                if last:
                    project_out(last, n - 1)
                if kind:
                    scores(n, 1, n - 2 if tail else None)
                elif tail:
                    experts(n - 2, 3)
                if mix:
                    turn_x(n - 1)
                if front:
                    turn_h(n + 1)
                if kind:
                    state_products(kind, n)
                if front:
                    project(front, n + 1, "qk")
                if mix:
                    router(n - 1)
                if kind:
                    heads(n, 0, n - 1 if mix else None)
                elif mix:
                    experts(n - 1, 0)
                if tail:
                    turn_a(n - 2, not mix)
                if kind:
                    heads(n, 1, n - 1 if mix else None)
                elif mix:
                    experts(n - 1, 1)
                if front:
                    turn_qk(n + 1)
                    project(front, n + 1, "v")
                if tail:
                    mix_out(n - 2)

            def between():
                pe.wait_ge(ld_b, 16 * 5)
                since(pe, at_qT, 2)
                since(pe, at_v, 2)
                since(pe, at_kT, 2)
                for k in range(KH):
                    for m, w in enumerate((wq_n, wk_n, wq_n, wk_n)):
                        for f in range(KH):
                            last = pe.matmul(S[:, 1024 * k + D * m + P * f:1024 * k + D * m + P * f + P],
                                             w[:, f, P * k:P * k + P], bd[:, m, :], start=True, stop=True)
                last.then_inc(s_fold, 1)
                pe.wait_ge(s_blo, 1)
                pe.wait_ge(s_bhi, 1)
                pe.wait_ge(s_elo, 2)
                pe.wait_ge(s_be, 2)

            pe.wait_ge(s_tern, 1)
            turn_h(0)
            project("a", 0, "qk")
            project("a", 0, "v")
            turn_qk(0)
            pe.wait_ge(s_tern, 2)
            steps(pe, step, between)

        @block.vector
        def _(dve):
            dve.wait_ge(ld_sm, 16)
            dve.tensor_scalar(neg_s[:], sm[:, S_S:S_S + HEADS], -1.0, None, ALU.mult).then_inc(s_neg, 1)
            dve.tensor_scalar(neg_sf[:], sm[:, S_DECAY:S_DECAY + KH], -1.0, None, ALU.mult).then_inc(s_neg, 1)

            def mean_magnitude(m, loaded, w, count):
                dve.wait_ge(loaded, 16)
                dve.tensor_reduce(absum[:, m:m + 1], w[:].rearrange("p k n -> p (k n)"), AX.X, ALU.add,
                                  apply_absolute_value=True).then_inc(s_abs, 1)
                dve.wait_ge(s_sum, m + 1)
                dve.tensor_scalar(wmean[:, m:m + 1], (TA, TF)[m][:, 0:1], 1.0 / count, 1e-5, ALU.mult,
                                  ALU.max).then_inc(s_lt, 1)
                dve.wait_ge(s_lt, 2 * m + 1)
                dve.reciprocal(wscale[:, m:m + 1], wmean[:, m:m + 1]).then_inc(s_mean, 1)

            def ternary(m, src, width, dst):
                dve.wait_ge(s_scaled, m + 1)
                dve.tensor_scalar(tern_lt[:, 0:width], src, -0.5, None, ALU.is_lt).then_inc(s_lt, 1)
                dve.wait_ge(s_lt, 2 * m + 2)
                dve.scalar_tensor_tensor(out=dst, in0=src, scalar=0.5, in1=tern_lt[:, 0:width], op0=ALU.is_gt,
                                         op1=ALU.subtract).then_inc(s_tern, 1)

            def tile_of(kind, n):
                src, slot = (xs, n) if kind == "a" else (xf, n - NT)
                return src[:, slot, :] if isinstance(slot, int) else src[:, bass.ds(slot, 1), :]

            def prep(kind, n):
                xt = tile_of(kind, n)
                dve.bn_stats(st_a[:], xt).then_inc(at_st, 1)
                since(dve, at_st, n + 1)
                dve.sem_inc(passed, 1)
                dve.bn_aggr(mv_a[:], st_a[:]).then_inc(at_mv, 1)
                since(dve, at_mv, n + 1)
                if kind == "a":
                    dve.tensor_scalar(var_a[:], mv_a[:, 1:2], 1.0 + EPS32, LN_EPS * EPS32, ALU.mult,
                                      ALU.add).then_inc(at_u, 1)
                    since(dve, at_hT, n)
                    dve.scalar_tensor_tensor(out=hn[:], in0=xt, scalar=mv_a[:, 0:1], in1=rw[:, R_QKVN:R_QKVN + D],
                                             op0=ALU.subtract, op1=ALU.mult).then_inc(at_h, 1)
                else:
                    dve.tensor_scalar(var_a[:], mv_a[:, 1:2], LN_EPS, None, ALU.add).then_inc(at_u, 1)
                    since(dve, at_hT, n)
                    dve.tensor_scalar(hn[:], xt, mv_a[:, 0:1], None, ALU.subtract).then_inc(at_h, 1)

            def lo_h(n):
                since(dve, at_hi, n + 1)
                dve.tensor_tensor(h_lo[:], S[:, 0:D], h_hi[:].bitcast(F32), ALU.subtract).then_inc(at_lo, 1)

            def features(n):
                since(dve, at_rs, n + 1)
                since(dve, at_proj, n + 1)
                dve.scalar_tensor_tensor(out=f1[:], in0=S[:, 0:512], scalar=rs_a[:, 0:1], in1=rw[:, R_B1:R_B1 + 512],
                                         op0=ALU.mult, op1=ALU.add)
                dve.scalar_tensor_tensor(out=f2[:], in0=S[:, 512:1024], scalar=rs_a[:, 0:1],
                                         in1=rw[:, R_B2:R_B2 + 512], op0=ALU.mult, op1=ALU.add).then_inc(at_f, 1)
                since(dve, at_f, n - NT + 1)
                dve.tensor_tensor(qk[:, D:2 * D], f1[:, D:2 * D], f2[:, D:2 * D], ALU.mult).then_inc(at_qk, 1)

            def even_odd_k(n):
                since(dve, at_turned, 2 * n + 2)
                dve.tensor_tensor(kT[:].rearrange("p e k t -> p e (k t)"),
                                  S[:, 0:D].unsqueeze(1).to_broadcast([P, 2, D]),
                                  c[:, C_EVEN:C_EVEN + 2].unsqueeze(2).to_broadcast([P, 2, D]),
                                  ALU.mult).then_inc(at_kT, 1)

            def mask(kind, n, half):
                if True:
                    since(dve, at_sc, 2 * n + 1 + half)
                    m = (decay[:, 8 * half:8 * half + 8, :] if kind == "a" else
                         causal.unsqueeze(1).to_broadcast([P, 8, P]))
                    dve.tensor_tensor(pr[:, 8 * half:8 * half + 8, :],
                                      S[:, 1024 * half:1024 * half + 1024].rearrange("p (s t) -> p s t", t=P), m,
                                      ALU.mult).then_inc(at_p, 1)

            def outputs(kind, n):
                if kind == "a":
                    since(dve, at_ocopy, n + 1)
                    dve.tensor_tensor(z2[:], o_sb[:], norm2[:], ALU.mult).then_inc(at_z2, 1)
                    dve.tensor_tensor(z1[:], o_sb[:], rw[:, R_NORM:R_NORM + D], ALU.mult).then_inc(at_z1, 1)
                else:
                    since(dve, at_sq, n + 1)
                    dve.tensor_reduce(u2[:], sq[:].rearrange("p (h d) -> p h d", d=DH), AX.X, ALU.add).then_inc(at_u1, 1)
                    since(dve, at_u1, n + 1)
                    dve.tensor_scalar(u2[:], u2[:], 1.0 / DH, HEAD_EPS / QK_SCALE ** 2, ALU.mult,
                                      ALU.add).then_inc(at_u2, 1)

            def output_scales(kind, n):
                if kind == "a":
                    since(dve, at_sq, n + 1)
                    dve.tensor_scalar(u1[:], sums[:, 0:1], EPS32 / D, EPS32 * NORM_EPS / QK_SCALE ** 2, ALU.mult,
                                      ALU.add).then_inc(at_u1, 1)
                    since(dve, s_sq2, n + 1)
                    since(dve, at_u1, n + 1)
                    dve.scalar_tensor_tensor(out=u2[:, 0:1], in0=sums[:, 1:2], scalar=1.0 / D, in1=u1[:],
                                             op0=ALU.mult, op1=ALU.add).then_inc(at_u2, 1)
                else:
                    since(dve, at_r2, n + 1)
                    dve.tensor_tensor(z2[:].rearrange("p (h d) -> p h d", d=DH),
                                      TA[:, 0:D].rearrange("p (h d) -> p h d", d=DH),
                                      r2[:].unsqueeze(2).to_broadcast([P, HEADS, DH]), ALU.mult).then_inc(at_z2, 1)

            def add_state(kind, n):
                since(dve, at_sbd, n + 1)
                since(dve, at_kv, n + 1)
                if kind == "a":
                    for f in range(KH):
                        last = dve.scalar_tensor_tensor(
                            out=state_a[:, f, :], in0=state_a[:, f, :], scalar=lam_p[:, f:f + 1],
                            in1=TA[:, D + P * f:D + P * f + P], op0=ALU.mult, op1=ALU.add)
                    last.then_inc(at_state, 1)
                else:
                    dve.tensor_tensor(state_b[:], state_b[:], TA[:, D:2 * D].rearrange("p (f t) -> p f t", f=KH),
                                      ALU.add).then_inc(at_state, 1)

            def lo_z(n):
                since(dve, at_zhi, n + 1)
                dve.tensor_tensor(z_lo[:], TA[:, 0:D], z_hi[:].bitcast(F32), ALU.subtract).then_inc(at_zlo, 1)

            def residual_a(kind, n):
                xt = tile_of(kind, n)
                since(dve, f_xr, n)
                since(dve, at_y, n + 1)
                if kind == "a":
                    since(dve, at_r2, n + 1)
                    dve.scalar_tensor_tensor(out=xc[:], in0=TA[:, D:2 * D], scalar=r2m[:, 0:1], in1=xt,
                                             op0=ALU.mult, op1=ALU.add).then_inc(at_x, 1)
                else:
                    dve.tensor_tensor(xc[:], TA[:, D:2 * D], xt, ALU.add).then_inc(at_x, 1)

            def stats_x(u):
                since(dve, at_x, u + 1)
                dve.bn_stats(st_f[:], xc[:]).then_inc(f_st, 1)
                since(dve, f_st, u + 1)
                dve.sem_inc(passed, 1)
                dve.bn_aggr(mv_f[:], st_f[:]).then_inc(f_mv, 1)
                since(dve, f_mv, u + 1)
                dve.tensor_scalar(var_f[:], mv_f[:, 1:2], LN_EPS, None, ALU.add).then_inc(f_u, 1)

            def norm_x(u):
                since(dve, f_T, u)
                since(dve, f_rs, u + 1)
                dve.tensor_scalar(xn[:], xc[:], mv_f[:, 0:1], rs_f[:, 0:1], ALU.subtract, ALU.mult).then_inc(f_xn, 1)

            def lo_x(u):
                since(dve, f_hi, u + 1)
                dve.tensor_tensor(x_lo[:], TF[:, D:2 * D], x_hi[:].bitcast(F32), ALU.subtract).then_inc(f_lo, 1)

            def choose(u):
                since(dve, f_lg, u + 1)
                dve.tensor_tensor(lg[:], TF[:, D:D + E], rw[:, R_RB:R_RB + E], ALU.add).then_inc(f_g, 1)
                since(dve, f_g, G_STEPS * u + 1)
                dve.sem_inc(passed, 1)
                dve.max(m8[:], lg[:]).then_inc(f_g, 1)
                since(dve, f_g, G_STEPS * u + 2)
                dve.tensor_tensor(dl[:], m8[:, 0:1], m8[:, 1:2], ALU.subtract).then_inc(f_d, 1)
                dve.max_index(ix[:], m8[:], lg[:]).then_inc(f_g, 1)
                since(dve, f_g, G_STEPS * u + 3)
                dve.tensor_copy(ixf[:], ix[:, 0:2]).then_inc(f_g, 1)
                since(dve, f_th, u + 1)
                dve.tensor_scalar(g12[:, 0:1], th[:], 0.5, 0.5, ALU.mult, ALU.add)
                dve.tensor_scalar(g12[:, 1:2], th[:], -0.5, 0.5, ALU.mult, ALU.add).then_inc(f_g, 1)
                since(dve, f_g, G_STEPS * u + 5)
                for i in range(2):
                    dve.tensor_scalar(oh[:, i, :], c[:, C_IOTA:C_IOTA + E], ixf[:, i:i + 1], g12[:, i:i + 1],
                                      ALU.is_equal, ALU.mult).then_inc(f_g, 1)
                since(dve, f_g, G_STEPS * u + 7)
                dve.tensor_tensor(gates[:], oh[:, 0, :], oh[:, 1, :], ALU.add).then_inc(f_g, 1)
                since(dve, f_g, G_STEPS * u + 8)

            def combine(u, g):
                since(dve, f_gelu, GROUPS * u + g + 1)
                for e in (2 * g, 2 * g + 1):
                    h = hb[:, g, D * (e % 2):D * (e % 2) + D]
                    if e == 0:
                        since(dve, f_aT, u)
                        dve.tensor_scalar(acc[:, 0, :], h, gates[:, 0:1], None, ALU.mult).then_inc(f_acc, 1)
                    else:
                        since(dve, f_acc, E * u + e)
                        dve.scalar_tensor_tensor(out=acc[:, e % 2, :], in0=h, scalar=gates[:, e:e + 1],
                                                 in1=acc[:, (e + 1) % 2, :], op0=ALU.mult, op1=ALU.add).then_inc(f_acc, 1)

            def lo_a(u):
                since(dve, f_ahi, u + 1)
                dve.tensor_tensor(a_lo[:], TF[:, 0:D], a_hi[:].bitcast(F32), ALU.subtract).then_inc(f_alo, 1)

            def residual_f(u):
                xt = xf[:, u, :] if isinstance(u, int) else xf[:, bass.ds(u, 1), :]
                since(dve, f_xr, u + 1)
                since(dve, f_y, u + 1)
                dve.tensor_tensor(xt, TF[:, 0:D], xr[:], ALU.add).then_inc(f_x, 1)

            def step(n, kind, last, front, mix, tail):
                if front:
                    prep(front, n + 1)
                if last:
                    lo_z(n - 1)
                    residual_a(last, n - 1)
                    stats_x(n - 1)
                if kind:
                    mask(kind, n, 0)
                if last:
                    norm_x(n - 1)
                if tail:
                    combine(n - 2, 2)
                if mix:
                    lo_x(n - 1)
                if front:
                    lo_h(n + 1)
                if kind:
                    add_state(kind, n)
                    mask(kind, n, 1)
                if tail:
                    combine(n - 2, 3)
                if front == "b":
                    features(n + 1)
                if mix:
                    choose(n - 1)
                    combine(n - 1, 0)
                if tail:
                    lo_a(n - 2)
                if kind:
                    outputs(kind, n)
                if front:
                    even_odd_k(n + 1)
                if kind:
                    output_scales(kind, n)
                if mix:
                    combine(n - 1, 1)
                if tail:
                    residual_f(n - 2)

            def between():
                dve.wait_ge(s_ehi, 1)
                dve.tensor_tensor(we_lo[:, 0, :], we_f[:, 0, :], we_hi[:, 0, :].bitcast(F32),
                                  ALU.subtract).then_inc(s_elo, 1)
                dve.wait_ge(ld_b, 16 * 5)
                dve.tensor_scalar(wo_s[:], wo_f[:], sm[:, S_HNORM:S_HNORM + 1], None, ALU.mult).then_inc(s_wos, 1)
                dve.wait_ge(s_be, 1)
                dve.scalar_tensor_tensor(out=be[0:2, :], in0=be[0:2, :].bitcast(F32),
                                         scalar=c[0:2, C_SECOND:C_SECOND + 1], in1=be_f[:], op0=ALU.mult,
                                         op1=ALU.add).then_inc(s_be, 1)
                dve.wait_ge(s_bhi, 1)
                dve.tensor_tensor(wr_lo[:], sm[:, S_ROUTER:S_ROUTER + KH * E].rearrange("p (k e) -> p k e", k=KH),
                                  wr_hi[:].bitcast(F32), ALU.subtract)
                dve.tensor_tensor(wout_lo[:], wout_f[:], wout_hi[:].bitcast(F32), ALU.subtract)
                dve.tensor_tensor(wb_lo[:, :, 4 * D:5 * D], wv_f[:], wb_hi[:, :, 4 * D:5 * D].bitcast(F32),
                                  ALU.subtract)
                dve.tensor_tensor(wb_lo[:, :, 0:4 * D], S[:].rearrange("p (k n) -> p k n", k=KH),
                                  wb_hi[:, :, 0:4 * D].bitcast(F32), ALU.subtract)
                dve.wait_ge(s_wos, 1)
                dve.tensor_tensor(wo_lo[:], wo_s[:], wo_hi[:].bitcast(F32), ALU.subtract).then_inc(s_blo, 1)
                dve.wait_ge(ld_rows, 16)

            mean_magnitude(0, ld_wqkv, wqkv_f, 3 * D * D)
            dve.wait_ge(ld_x0, 16)
            dve.wait_ge(ld_norms, 16)
            prep("a", 0)
            ternary(0, tern_tmp, KH * 3 * D, wqkv_t[:].rearrange("p k n -> p (k n)"))
            mean_magnitude(1, ld_wproj, wproj_f, D * D)
            lo_h(0)
            ternary(1, tern2, KH * D, wproj_t[:].rearrange("p k n -> p (k n)"))
            even_odd_k(0)
            dve.wait_ge(s_exp, 1)
            dve.tensor_tensor(decay[:], decay[:], causal.unsqueeze(1).to_broadcast([P, SLOTS, P]),
                              ALU.mult).then_inc(s_decay, 1)
            dve.wait_ge(s_decay, 1)
            dve.wait_ge(s_norm2, 1)
            dve.wait_ge(ld_x, 16)
            steps(dve, step, between)


def halves(a):
    return np.ascontiguousarray(a.reshape(KH, P, -1).transpose(1, 0, 2))


def constants():
    p, t = np.arange(P)[:, None], np.arange(P)[None, :]
    a = np.zeros((P, C_END), np.float32)
    a[:, C_ID:C_ID + P] = p == t
    a[:, C_ONE:C_ONE + P] = 1
    a[:, C_CAUSAL:C_CAUSAL + P] = p <= t
    a[:, C_DIFF:C_DIFF + P] = np.maximum(t - p, 0)
    a[:, C_BLOCK:C_BLOCK + P] = p // DH == t // DH
    a[:, C_TT:C_TT + P] = t
    a[0:2, C_PAIR:C_PAIR + P] = 1
    a[:, C_IOTA:C_IOTA + E] = np.arange(E)
    a[:, C_EVEN:C_EVEN + 1] = p // DH % 2 == 0
    a[:, C_ODD:C_ODD + 1] = p // DH % 2 == 1
    a[1, C_SECOND] = -1
    a[:, C_REV:C_REV + 1] = P - p
    return a


def kernel(**inputs):
    import concourse.bacc as bacc
    from concourse.bass_utils import run_bass_kernel_spmd

    a = {k: np.asarray(w) for k, w in inputs.items()}
    A, B, F = "L0_attn_a_", "L0_attn_b_", "L0_ffn_"
    small = np.zeros((P, S_END), np.float32)
    small[:, S_DECAY:S_DECAY + KH] = np.repeat(a[A + "s"], DH).reshape(KH, P).T
    small[:, S_HNORM] = np.tile(a[B + "norm_w"], P // DH)
    small[:, S_ROUTER:S_S] = halves(a[F + "router_w"]).reshape(P, KH * E)
    small[:, S_S:S_END] = a[A + "s"]
    rows = np.concatenate([
        a[A + "qkv_norm_w"], a[A + "norm_w"], a[A + "proj_norm_w"],
        np.tile(a[B + "fq1_b"], HEADS), np.tile(a[B + "fk1_b"], HEADS),
        np.tile(a[B + "fq2_b"], HEADS), np.tile(a[B + "fk2_b"], HEADS),
        a[F + "out_b"], a[F + "router_b"]])[None, :]
    bdiag = np.zeros((P, 4, P), np.float32)
    for m, name in enumerate(("fq1_w", "fk1_w", "fq2_w", "fk2_w")):
        for h in range(P // DH):
            bdiag[DH * h:DH * h + DH, m, DH * h:DH * h + DH] = a[B + name].T
    experts = a[F + "expert_w"].transpose(1, 0, 2).reshape(D, E * D)
    arrays = {
        "x": a[A + "x"], "cst": constants(), "small": small, "rows": rows,
        "wqkv": halves(a[A + "qkv_w"].T), "wproj": halves(a[A + "proj_w"].T), "bdiag": bdiag,
        "wq": halves(a[B + "wq"]), "wk": halves(a[B + "wk"]), "wv": halves(a[B + "wv"].T),
        "wo": halves(a[B + "wo"].T), "wexp": halves(experts),
        "bexp": np.repeat(a[F + "expert_b"].reshape(1, E * D), 2, axis=0), "wout": halves(a[F + "out_w"]),
    }
    arrays = {f"in_{k}": np.ascontiguousarray(w) for k, w in arrays.items()}
    nc = bacc.Bacc("TRN2", target_bir_lowering=False, num_devices=1)
    args = [nc.dram_tensor(k, w.shape, mybir.dt.from_np(w.dtype), kind="ExternalInput").ap() for k, w in arrays.items()]
    args.append(nc.dram_tensor("out_0", (1, T, D), F32, kind="ExternalOutput").ap())
    build(nc, *args)
    r = run_bass_kernel_spmd(nc, [arrays], core_ids=[0])
    return r.results[0]["out_0"]
```

```python
from contextlib import ExitStack

import numpy as np

import concourse.bass as bass
from concourse import mybir

F32 = mybir.dt.float32
F32R = mybir.dt.float32r
U32 = mybir.dt.uint32
ALU = mybir.AluOpType
ACT = mybir.ActivationFunctionType
AX = mybir.AxisListType

P = 128
T = 1024
D = 256
KH = D // P
HEADS = 16
DH = D // HEADS
NT = T // P
E = 8
GROUPS = E * D // 512
SLOTS = HEADS
EPS32 = float(np.finfo(np.float32).eps)
LN_EPS = 1e-5
NORM_EPS = 1e-6
HEAD_EPS = 1e-5
QK_SCALE = DH ** -0.5
ROUND = 1.5 * 2.0 ** 23

C_ID, C_DIFF, C_TT, C_CAUSAL, C_BLOCK, C_IOTA, C_EVEN, C_ODD, C_SECOND, C_REV, C_GROUP, C_END = (
    0, 128, 256, 384, 512, 640, 648, 649, 650, 651, 652, 656)
S_DECAY, S_HNORM, S_ROUTER, S_S, S_END = 0, 2, 3, 19, 35
R_QKVN, R_NORM, R_PROJN, R_B1, R_B2, R_OUTB, R_RB, R_END = (
    0, 256, 512, 768, 1280, 1792, 2048, 2056)


def head_of(j, i):
    return 8 * (i // 2) + 2 * j + i % 2


def build(nc, x, cst, small, rows, wqkv, wproj, bdiag, wq, wk, wv, wo, wexp, bexp, wout, out):
    with ExitStack() as ctx:
        def sb(name, shape, dt=F32):
            return ctx.enter_context(nc.sbuf_tensor(name, shape, dt))

        def sem(name):
            return ctx.enter_context(nc.semaphore(name))

        def psum(name, shape):
            return ctx.enter_context(nc.psum_tensor(name, shape, F32))

        S = psum("S", [P, 4 * 512])
        TA = psum("TA", [P, 512])
        TF = psum("TF", [P, 512])
        EX = psum("EX", [P, 2, 512])

        xs = sb("xs", [P, NT, D])
        c = sb("c", [P, C_END])
        sm = sb("sm", [P, S_END])
        rw = sb("rw", [P, R_END])
        wqkv_f = sb("wqkv_f", [P, KH, 3 * D])
        wproj_f = sb("wproj_f", [P, KH, D])
        wqkv_t = sb("wqkv_t", [P, KH, 3 * D], F32R)
        wproj_t = sb("wproj_t", [P, KH, D], F32R)
        bd = sb("bd", [P, 4, P])
        norm2 = sb("norm2", [P, D])
        wq_n = sb("wq_n", [P, KH, D])
        wk_n = sb("wk_n", [P, KH, D])
        wv_f = sb("wv_f", [P, KH, D])
        wo_f = sb("wo_f", [P, KH, D])
        wo_s = sb("wo_s", [P, KH, D])
        wb_hi = sb("wb_hi", [P, KH, 5 * D], F32R)
        wb_lo = sb("wb_lo", [P, KH, 5 * D], F32R)
        wo_hi = sb("wo_hi", [P, KH, D], F32R)
        wo_lo = sb("wo_lo", [P, KH, D], F32R)
        we_f = sb("we_f", [P, KH, E * D])
        xf = we_f[:].rearrange("p k n -> p (k n)").rearrange("p (t d) -> p t d", d=D)
        we_hi = sb("we_hi", [P, KH, E * D], F32R)
        we_lo = sb("we_lo", [P, KH, E * D], F32R)
        ones = sb("ones", [P, P])
        be_f = sb("be_f", [2 * GROUPS, 512])
        be = sb("be", [P, 512], F32R)
        pair = sb("pair", [P, GROUPS, P], F32R)
        wout_f = sb("wout_f", [P, KH, D])
        wout_hi = sb("wout_hi", [P, KH, D], F32R)
        wout_lo = sb("wout_lo", [P, KH, D], F32R)
        wr = sb("wr", [P, KH, 2 * E], F32R)
        absum = sb("absum", [P, KH + 1])
        wmean = sb("wmean", [P, 2])
        wscale = sb("wscale", [P, 2])
        neg_s = sb("neg_s", [P, HEADS])
        neg_sf = sb("neg_sf", [P, KH])
        mhalf = sb("mhalf", [P, HEADS])
        decay = sb("decay", [P, SLOTS, P])
        lam_q = sb("lam_q", [P, KH, P])
        lam_k = sb("lam_k", [P, HEADS])
        lam_p = sb("lam_p", [P, KH])

        st_a = sb("st_a", [P, 6])
        mv_a = sb("mv_a", [P, 2])
        var_a = sb("var_a", [P, 1])
        rs_a = sb("rs_a", [P, 1])
        hn = sb("hn", [P, D])
        h_hi = sb("h_hi", [P, D], F32R)
        h_lo = sb("h_lo", [P, D], F32R)
        f1 = sb("f1", [P, 512])
        f2 = sb("f2", [P, 512])
        qk = sb("qk", [P, 512])
        v = sb("v", [P, D])
        qT = sb("qT", [P, KH, P])
        qTl = sb("qTl", [P, KH, P])
        kT = sb("kT", [P, 2, KH, P])
        o_sb = sb("o_sb", [P, D])
        kl = sb("kl", [P, D])
        pr = sb("pr", [P, SLOTS, P])
        state_a = sb("state_a", [P, KH, P])
        state_b = sb("state_b", [P, KH, P])
        sbd_a = sb("sbd_a", [P, KH, P])
        sbd_b = sb("sbd_b", [P, KH, P])
        z1 = sb("z1", [P, D])
        z2 = sb("z2", [P, D])
        sq = sb("sq", [P, D])
        sq2 = sb("sq2", [P, D])
        sums = sb("sums", [P, 2])
        u1 = sb("u1", [P, 1])
        u2 = sb("u2", [P, HEADS])
        r2 = sb("r2", [P, HEADS])
        r2m = sb("r2m", [P, 1])
        z_hi = sb("z_hi", [P, D], F32R)
        z_lo = sb("z_lo", [P, D], F32R)
        xc = sb("xc", [P, D])

        st_f = sb("st_f", [P, 6])
        mv_f = sb("mv_f", [P, 2])
        var_f = sb("var_f", [P, 1])
        rs_f = sb("rs_f", [P, 1])
        xn = sb("xn", [P, D])
        xr = sb("xr", [P, D])
        x_hi = sb("x_hi", [P, D], F32R)
        x_lo = sb("x_lo", [P, D], F32R)
        lg1 = sb("lg1", [P, E])
        lg = sb("lg", [P, E])
        m8 = sb("m8", [P, E])
        ix = sb("ix", [P, E], U32)
        ixf = sb("ixf", [P, 2])
        dl = sb("dl", [P, 1])
        th = sb("th", [P, 1])
        g12 = sb("g12", [P, 2])
        oh = sb("oh", [P, 2, E])
        gates = sb("gates", [P, E])
        hb = sb("hb", [P, GROUPS, 512])
        acc = sb("acc", [P, 2, D])
        tern = hb[:].rearrange("p g n -> p (g n)")[:, 0:KH * 3 * D].rearrange("p (k n) -> p k n", k=KH)
        tern2 = acc
        a_hi = sb("a_hi", [P, D], F32R)
        a_lo = sb("a_lo", [P, D], F32R)

        ld_c, ld_sm, ld_rows, ld_x0, ld_x = sem("ld_c"), sem("ld_sm"), sem("ld_rows"), sem("ld_x0"), sem("ld_x")
        ld_norms = sem("ld_norms")
        ld_wqkv0, ld_wqkv1, ld_wproj, ld_fold, ld_b, ld_e, ld_be, ld_wout = (
            sem("ld_wqkv0"), sem("ld_wqkv1"), sem("ld_wproj"), sem("ld_fold"), sem("ld_b"), sem("ld_e"),
            sem("ld_be"), sem("ld_wout"))
        s_abs, s_sum, s_mean, s_round, s_tern = sem("s_abs"), sem("s_sum"), sem("s_mean"), sem("s_round"), sem("s_tern")
        s_neg, s_exp, s_decay0, s_decay1, s_fill = (
            sem("s_neg"), sem("s_exp"), sem("s_decay0"), sem("s_decay1"), sem("s_fill"))
        s_fold, s_bhi, s_blo, s_wos = sem("s_fold"), sem("s_bhi"), sem("s_blo"), sem("s_wos")
        s_ehi, s_elo, s_be, s_mhi, s_mlo = sem("s_ehi"), sem("s_elo"), sem("s_be"), sem("s_mhi"), sem("s_mlo")
        s_ones = sem("s_ones")
        at_st, at_mv, at_u, at_rs, at_h, at_hT, at_hi, at_lo = (
            sem("at_st"), sem("at_mv"), sem("at_u"), sem("at_rs"), sem("at_h"), sem("at_hT"), sem("at_hi"), sem("at_lo"))
        at_proj, at_projv, at_f, at_qk, at_v, at_turned, at_qT, at_kT, at_ql, at_kl = (
            sem("at_proj"), sem("at_projv"), sem("at_f"), sem("at_qk"), sem("at_v"), sem("at_turned"), sem("at_qT"),
            sem("at_kT"), sem("at_ql"), sem("at_kl"))
        at_sc, at_p, at_kv, at_ocopy, at_o, at_state, at_sbd = (
            sem("at_sc"), sem("at_p"), sem("at_kv"), sem("at_ocopy"), sem("at_o"), sem("at_state"), sem("at_sbd"))
        at_sq, at_z1, at_u1, at_u2, at_r2, at_z2, at_zT, at_zhi, at_zlo, at_y, at_x = (
            sem("at_sq"), sem("at_z1"), sem("at_u1"), sem("at_u2"), sem("at_r2"), sem("at_z2"), sem("at_zT"),
            sem("at_zhi"), sem("at_zlo"), sem("at_y"), sem("at_x"))
        f_st, f_mv, f_u, f_rs, f_xn, f_xr, f_T, f_hi, f_lo, f_lg = (
            sem("f_st"), sem("f_mv"), sem("f_u"), sem("f_rs"), sem("f_xn"), sem("f_xr"), sem("f_T"), sem("f_hi"),
            sem("f_lo"), sem("f_lg"))
        f_g, f_d, f_th, f_ex, f_gelu, f_acc, f_aT, f_ahi, f_alo, f_y, f_x = (
            sem("f_g"), sem("f_d"), sem("f_th"), sem("f_ex"), sem("f_gelu"), sem("f_acc"), sem("f_aT"), sem("f_ahi"),
            sem("f_alo"), sem("f_y"), sem("f_x"))
        passed, s_pow, s_pow2, s_sq2 = sem("passed"), sem("s_pow"), sem("s_pow2"), sem("s_sq2")
        st_out, s_norm2, f_l1 = sem("st_out"), sem("s_norm2"), sem("f_l1")

        ident = c[:, C_ID:C_ID + P]
        causal = c[:, C_CAUSAL:C_CAUSAL + P]
        out_t = out[0].rearrange("(t p) d -> t p d", p=P)
        x_t = x[0].rearrange("(t p) d -> p t d", p=P)

        def at(n, k):
            return isinstance(n, int) and n == k

        G_STEPS = 8

        def since(eng, s, n):
            if not isinstance(n, int) or n > 0:
                eng.wait_ge(s, n)

        def steps(eng, step):
            step(0, "a", None, "a", False, False)
            step(1, "a", "a", "a", True, False)
            with eng.Fori(2, NT - 1) as n:
                step(n, "a", "a", "a", True, True)
            step(NT - 1, "a", "a", "b", True, True)
            step(NT, "b", "a", "b", True, True)
            with eng.Fori(NT + 1, 2 * NT - 1) as n:
                step(n, "b", "b", "b", True, True)
            step(2 * NT - 1, "b", "b", None, True, True)
            step(2 * NT, None, "b", None, True, True)
            step(2 * NT + 1, None, None, None, False, True)

        block = ctx.enter_context(nc.Block())

        @block.sync
        def _(sp):
            for k in range(KH):
                sp.dma_start(wqkv_f[:, k, :], wqkv[:, k, :]).then_inc((ld_wqkv0, ld_wqkv1)[k], 16)
            sp.dma_start(sm[:], small).then_inc(ld_sm, 16)
            sp.dma_start(xs[:, 0, :], x_t[:, 0, :]).then_inc(ld_x0, 16)
            sp.dma_start(rw[:, 0:R_B1], rows[:, 0:R_B1].to_broadcast([P, R_B1])).then_inc(ld_norms, 16)
            sp.dma_start(c[:], cst).then_inc(ld_c, 16)
            sp.dma_start(wproj_f[:], wproj).then_inc(ld_wproj, 16)
            for to, w in ((bd, bdiag), (wq_n, wq), (wk_n, wk)):
                sp.dma_start(to[:], w).then_inc(ld_fold, 16)
            sp.dma_start(xs[:, 1:NT, :], x_t[:, 1:NT, :]).then_inc(ld_x, 16)
            sp.dma_start(we_f[:], wexp).then_inc(ld_e, 16)
            sp.dma_start(be_f[:], bexp).then_inc(ld_be, 16)
            sp.dma_start(wout_f[:], wout).then_inc(ld_wout, 16)
            sp.dma_start(rw[:, R_B1:R_END], rows[:, R_B1:R_END].to_broadcast([P, R_END - R_B1])).then_inc(ld_rows, 16)
            for to, w in ((wv_f, wv), (wo_f, wo)):
                sp.dma_start(to[:], w).then_inc(ld_b, 16)
            with sp.Fori(0, NT) as t:
                to = out_t[bass.ds(t, 1)]
                tile = xf[:, bass.ds(t + NT, 1), :]
                sp.wait_ge(f_x, t + NT + 1)
                sp.dma_start(to, tile).then_inc(st_out, 16)
            sp.wait_ge(st_out, 16 * NT)

        @block.gpsimd
        def _(pool):
            pool.memset(ones[:], 1.0).then_inc(s_ones, 1)
            pool.memset(mhalf[:], -0.5)
            pool.memset(state_a[:], 0.0)
            pool.memset(state_b[:], 0.0)
            pool.memset(sbd_a[:], 0.0)
            pool.memset(sbd_b[:], 0.0).then_inc(at_sbd, 1)
            pool.memset(be[:].bitcast(F32), 0.0).then_inc(s_fill, 1)
            pool.wait_ge(s_fill, 1)

            def start(kind, n):
                since(pool, at_v, n)
                since(pool, at_u, n + 1)
                if kind == "a":
                    pool.tensor_tensor(rs_a[:], var_a[:], mhalf[:, 0:1], ALU.pow).then_inc(s_pow, 1)
                    pool.wait_ge(s_pow, n + 1)
                    pool.tensor_tensor(rs_a[:], rs_a[:], wmean[:, 0:1], ALU.mult).then_inc(at_rs, 1)
                else:
                    pool.tensor_tensor(rs_a[:], var_a[:], mhalf[:, 0:1], ALU.pow).then_inc(at_rs, 1)

            def decayed_k(n):
                since(pool, at_qk, 2 * n + 2)
                pool.tensor_tensor(kl[:].rearrange("p (h d) -> p h d", d=DH),
                                   qk[:, D:2 * D].rearrange("p (h d) -> p h d", d=DH),
                                   lam_k[:].unsqueeze(2).to_broadcast([P, HEADS, DH]), ALU.mult).then_inc(at_kl, 1)

            def decayed_q(n):
                since(pool, at_qT, n + 1)
                pool.tensor_tensor(qTl[:], qT[:], lam_q[:], ALU.mult).then_inc(at_ql, 1)

            def products(n):
                since(pool, at_f, n - NT + 1)
                pool.tensor_tensor(qk[:, 0:D], f1[:, 0:D], f2[:, 0:D], ALU.mult).then_inc(at_qk, 1)

            def norms(kind, n):
                if kind == "a":
                    since(pool, at_u2, n + 1)
                    pool.tensor_tensor(r2[:, 0:1], u2[:, 0:1], mhalf[:, 0:1], ALU.pow).then_inc(s_pow2, 1)
                    pool.wait_ge(s_pow2, n + 1)
                    pool.tensor_tensor(r2m[:], r2[:, 0:1], wmean[:, 1:2], ALU.mult).then_inc(at_r2, 1)
                else:
                    since(pool, at_u2, n + 1)
                    pool.tensor_tensor(r2[:], u2[:], mhalf[:], ALU.pow).then_inc(at_r2, 1)

            def own_heads(kind, n):
                since(pool, at_state, n + 1)
                state, sbd = (state_a, sbd_a) if kind == "a" else (state_b, sbd_b)
                pool.tensor_tensor(sbd[:], state[:], c[:, C_BLOCK:C_BLOCK + P].unsqueeze(1).to_broadcast([P, KH, P]),
                                   ALU.mult).then_inc(at_sbd, 1)

            def root_x(n):
                since(pool, f_u, n + 1)
                pool.tensor_tensor(rs_f[:], var_f[:], mhalf[:, 0:1], ALU.pow).then_inc(f_rs, 1)

            def biased_x(u):
                since(pool, f_x, u)
                pool.tensor_tensor(xr[:], xc[:], rw[:, R_OUTB:R_OUTB + D], ALU.add).then_inc(f_xr, 1)

            def step(n, kind, last, front, mix, tail):
                if front:
                    start(front, n + 1)
                if last:
                    root_x(n - 1)
                if kind:
                    own_heads(kind, n)
                if front == "a":
                    decayed_k(n + 1)
                if at(n, 0):
                    pool.wait_ge(s_ehi, 2)
                    pool.tensor_tensor(we_lo[:, 1, :], we_f[:, 1, :], we_hi[:, 1, :].bitcast(F32),
                                       ALU.subtract).then_inc(s_elo, 1)
                if front == "b":
                    products(n + 1)
                if kind:
                    norms(kind, n)
                if front == "a":
                    decayed_q(n + 1)
                if at(n, 1):
                    pool.wait_ge(ld_rows, 16)
                if mix:
                    biased_x(n - 1)

            pool.wait_ge(s_mean, 1)
            start("a", 0)
            pool.wait_ge(ld_norms, 16)
            pool.tensor_tensor(norm2[:], rw[:, R_NORM:R_NORM + D], rw[:, R_PROJN:R_PROJN + D],
                               ALU.mult).then_inc(s_norm2, 1)
            pool.wait_ge(s_exp, 1)
            pool.wait_ge(ld_c, 16)
            decayed_k(0)
            decayed_q(0)
            pool.wait_ge(s_exp, 3)
            pool.tensor_tensor(decay[:, 8:16, :], decay[:, 8:16, :], causal.unsqueeze(1).to_broadcast([P, 8, P]),
                               ALU.mult).then_inc(s_decay1, 1)
            pool.wait_ge(s_mean, 2)
            steps(pool, step)

        @block.scalar
        def _(act):
            act.wait_ge(ld_c, 16)
            act.wait_ge(s_neg, 2)
            act.activation(lam_k[:], neg_s[:], ACT.Exp, scale=c[:, C_REV:C_REV + 1])
            for k in range(KH):
                act.activation(lam_q[:, k, :], c[:, C_TT:C_TT + P], ACT.Exp, scale=neg_sf[:, k:k + 1])
            act.activation(lam_p[:], neg_sf[:], ACT.Exp, scale=float(P)).then_inc(s_exp, 1)

            def decays(j):
                for i in range(4):
                    h = head_of(j, i)
                    last = act.activation(decay[:, 4 * j + i, :], c[:, C_DIFF:C_DIFF + P], ACT.Exp,
                                          scale=neg_s[:, h:h + 1])
                if j % 2 == 1:
                    last.then_inc(s_exp, 1)

            def hi_h(n):
                since(act, at_hT, n + 1)
                act.activation(h_hi[:], S[:, 0:D], ACT.Copy).then_inc(at_hi, 1)

            def hi_x(u):
                since(act, f_T, u + 1)
                act.activation(x_hi[:], TF[:, D:2 * D], ACT.Copy).then_inc(f_hi, 1)

            def evac_qk(kind, n):
                since(act, at_rs, n + 1)
                if kind == "a":
                    since(act, at_proj, n + 1)
                    act.activation(qk[:, 0:D], S[:, 0:D], ACT.Copy, scale=rs_a[:, 0:1]).then_inc(at_qk, 1)
                    act.activation(qk[:, D:2 * D], S[:, D:2 * D], ACT.Copy, scale=rs_a[:, 0:1]).then_inc(at_qk, 1)

            def evac_v(n):
                since(act, at_projv, n + 1)
                act.activation(v[:], S[:, 2 * 512:2 * 512 + D], ACT.Copy, scale=rs_a[:, 0:1]).then_inc(at_v, 1)

            def evac_qT(n):
                since(act, at_turned, 2 * n + 1)
                act.activation(qT[:], S[:, 1536:1536 + D].rearrange("p (k t) -> p k t", k=KH), ACT.Copy).then_inc(at_qT, 1)

            def squares(kind, n):
                since(act, at_o, n + 1)
                if kind == "a":
                    act.activation(o_sb[:], TA[:, 0:D], ACT.Copy).then_inc(at_ocopy, 1)
                    since(act, at_ocopy, n + 1)
                    act.activation(sq[:], o_sb[:], ACT.Square, accum_out=sums[:, 0:1]).then_inc(at_sq, 1)
                else:
                    act.activation(sq[:], TA[:, 0:D], ACT.Square).then_inc(at_sq, 1)

            def squares_z(n):
                since(act, at_z1, n + 1)
                act.activation(sq2[:], z1[:], ACT.Square, accum_out=sums[:, 1:2]).then_inc(s_sq2, 1)

            def hi_z(n):
                since(act, at_zT, n + 1)
                act.activation(z_hi[:], TA[:, 0:D], ACT.Copy).then_inc(at_zhi, 1)

            def tanh(u):
                since(act, f_d, u + 1)
                act.activation(th[:], dl[:], ACT.Tanh, scale=0.5).then_inc(f_th, 1)

            def gelu(u, g):
                since(act, f_ex, GROUPS * u + g + 1)
                act.activation(hb[:, g, :], EX[:, g % 2, :], ACT.Gelu_apprx_tanh).then_inc(f_gelu, 1)

            def hi_a(u):
                since(act, f_aT, u + 1)
                act.activation(a_hi[:], TF[:, 0:D], ACT.Copy).then_inc(f_ahi, 1)

            def step(n, kind, last, front, mix, tail):
                if last:
                    hi_z(n - 1)
                if tail:
                    gelu(n - 2, 2)
                if front:
                    hi_h(n + 1)
                if tail:
                    gelu(n - 2, 3)
                if mix:
                    hi_x(n - 1)
                if front:
                    evac_qk(front, n + 1)
                if at(n, 2 * NT - 1):
                    squares(kind, n)
                if mix:
                    tanh(n - 1)
                    gelu(n - 1, 0)
                if tail:
                    hi_a(n - 2)
                if at(n, 0):
                    act.wait_ge(ld_e, 16)
                    for k in range(KH):
                        act.activation(we_hi[:, k, :], we_f[:, k, :], ACT.Copy).then_inc(s_ehi, 1)
                        if k == 0:
                            evac_qT(1)
                            folded_hi(1)
                if at(n, 1):
                    act.wait_ge(ld_b, 16 * 2)
                    act.activation(wb_hi[:, :, 4 * D:5 * D], wv_f[:], ACT.Copy)
                    act.wait_ge(s_wos, 1)
                    act.activation(wo_hi[:], wo_s[:], ACT.Copy).then_inc(s_bhi, 1)
                if front and not at(n, 0):
                    evac_qT(n + 1)
                if kind and not at(n, 2 * NT - 1):
                    squares(kind, n)
                if front:
                    evac_v(n + 1)
                if kind == "a":
                    squares_z(n)
                if mix:
                    gelu(n - 1, 1)

            def folded_hi(k):
                act.wait_ge(s_fold, k + 1)
                act.activation(wb_hi[:, k, 0:4 * D], EX[:].rearrange("p g n -> p (g n)"), ACT.Copy).then_inc(s_bhi, 1)

            def mixture_hi():
                act.wait_ge(ld_be, 16)
                act.wait_ge(s_fill, 1)
                act.activation(be[0:2 * GROUPS, :], be_f[:], ACT.Copy).then_inc(s_be, 1)
                act.activation(wr[:, :, 0:E], sm[:, S_ROUTER:S_ROUTER + KH * E].rearrange("p (k e) -> p k e", k=KH),
                               ACT.Copy)
                act.wait_ge(s_ones, 1)
                for g in range(GROUPS):
                    act.activation(pair[:, g, :], ones[:], ACT.Copy, scale=c[:, C_GROUP + g:C_GROUP + g + 1])
                act.wait_ge(ld_wout, 16)
                act.activation(wout_hi[:], wout_f[:], ACT.Copy).then_inc(s_mhi, 1)

            hi_h(0)
            decays(0)
            decays(1)
            evac_qk("a", 0)
            evac_v(0)
            evac_qT(0)
            decays(2)
            decays(3)
            act.preload_act_table(ACT.Gelu_apprx_tanh)
            folded_hi(0)
            mixture_hi()
            steps(act, step)

        @block.tensor
        def _(pe):
            pe.wait_ge(s_ones, 1)

            def sum_magnitudes(m):
                halves = range(KH) if m == 0 else (KH,)
                for i in halves:
                    pe.wait_ge(s_abs, i + 1)
                    last = pe.matmul((TA, TF)[m][:, 0:1], ones[:], absum[:, i:i + 1], start=(i == halves[0]),
                                     stop=(i == halves[-1]))
                last.then_inc(s_sum, 1)

            def fold(k, i):
                m, f = i // KH, i % KH
                last = pe.matmul(EX[:, m // 2, D * (m % 2) + P * f:D * (m % 2) + P * f + P],
                                 (wq_n, wk_n, wq_n, wk_n)[m][:, f, P * k:P * k + P], bd[:, m, :], start=True, stop=True)
                if i == 7:
                    last.then_inc(s_fold, 1)

            def turn_h(n):
                since(pe, at_h, n + 1)
                since(pe, at_p, 2 * n - 1)
                for k in range(KH):
                    last = pe.transpose(S[:, P * k:P * k + P], hn[:, P * k:P * k + P], ident)
                last.then_inc(at_hT, 1)

            def project(kind, n, part):
                if part == "qk":
                    since(pe, at_hi, n + 1)
                    since(pe, at_lo, n + 1)
                w_hi, w_lo, width = (wqkv_t, None, 3 * D) if kind == "a" else (wb_hi, wb_lo, 5 * D)
                passes = [(h_hi, w_hi), (h_lo, w_hi)] + ([(h_hi, w_lo)] if w_lo is not None else [])
                n0, n1, done = (0, width - D, at_proj) if part == "qk" else (width - D, width, at_projv)
                to = 0 if part == "qk" else 2 * 512 - n0
                for k in range(KH):
                    if at(n, 0) and part == "qk":
                        pe.wait_ge(s_tern, k + 1)
                    for i, (h, w) in enumerate(passes):
                        for c0 in range(n0, n1, 512):
                            c1 = min(c0 + 512, n1)
                            last = pe.matmul(S[:, to + c0:to + c1], h[:, P * k:P * k + P], w[:, k, c0:c1],
                                             start=(k == 0 and i == 0), stop=(k == KH - 1 and i == len(passes) - 1))
                last.then_inc(done, 1)

            def turn_qk(n):
                since(pe, at_qk, 2 * n + 2)
                since(pe, at_p, 2 * n)
                for base, m in ((1536, 0), (0, 1)):
                    for f in range(KH):
                        last = pe.transpose(S[:, base + P * f:base + P * f + P],
                                            qk[:, D * m + P * f:D * m + P * f + P], ident)
                    last.then_inc(at_turned, 1)

            def scores(n, half, u=None, before=None):
                if half == 0:
                    since(pe, at_qT, n + 1)
                    since(pe, at_kT, n + 1)
                else:
                    since(pe, at_v, n + 1)
                for m in range(8):
                    i, j = m // 2, 2 * half + m % 2
                    rows_j = slice(32 * j, 32 * j + 32)
                    last = pe.matmul(S[:, 512 * j + P * i:512 * j + P * i + P], kT[rows_j, i % 2, i // 2, :],
                                     qT[rows_j, i // 2, :], start=True, stop=True)
                    if m == 7:
                        last.then_inc(at_sc, 1)
                    elif u is not None:
                        expert(u, 2 + half, m)
                    if before and half == 0 and m == (3 if before == "a" else 7):
                        turn_z(n - 1)
                    if before and half == 1 and m == (1 if before == "a" else 2):
                        project_out(before, n - 1)

            def state_products(kind, n):
                since(pe, at_x, n)
                since(pe, at_sbd, n + 1)
                q, sbd = (qT, sbd_b) if kind == "b" else (qTl, sbd_a)
                if kind == "a":
                    since(pe, at_ql, n + 1)
                    since(pe, at_kl, n + 1)
                for f in range(KH):
                    pe.matmul(TA[:, P * f:P * f + P], q[:, f, :], sbd[:, f, :], start=(f == 0), stop=False,
                              skip_group_check=True)
                for f in range(KH):
                    lhs = qk[:, D + P * f:D + P * f + P] if kind == "b" else kl[:, P * f:P * f + P]
                    last = pe.matmul(TA[:, D + P * f:D + P * f + P], lhs, v[:, P * f:P * f + P], start=False, stop=True,
                                     skip_group_check=True)
                last.then_inc(at_kv, 1)

            def heads(n, half, u=None):
                if half == 0:
                    since(pe, at_state, n + 1)
                    if at(n, 0):
                        pe.wait_ge(s_bhi, 1)
                        pe.wait_ge(s_blo, 1)
                since(pe, at_p, 2 * n + 1 + half)
                for m in range(8):
                    j, i = 2 * half + m // 4, m % 4
                    h = head_of(j, i)
                    last = pe.matmul(TA[:, DH * h:DH * h + DH], pr[:, 4 * j + i, :], v[:, DH * h:DH * h + DH],
                                     start=False, stop=True, skip_group_check=True)
                    if m < 7 and u is not None:
                        expert(u, half, m)
                    if at(n, 0) and half == 0:
                        fold(1, m)
                if half == 1:
                    last.then_inc(at_o, 1)

            def turn_z(n):
                since(pe, at_z2, n + 1)
                for k in range(KH):
                    last = pe.transpose(TA[:, P * k:P * k + P], z2[:, P * k:P * k + P], ident)
                last.then_inc(at_zT, 1)

            def project_out(kind, n):
                since(pe, at_zhi, n + 1)
                since(pe, at_zlo, n + 1)
                if at(n, 0):
                    pe.wait_ge(s_tern, 2 * KH)
                w_hi, w_lo = (wproj_t, None) if kind == "a" else (wo_hi, wo_lo)
                passes = [(z_hi, w_hi), (z_lo, w_hi)] + ([(z_hi, w_lo)] if w_lo is not None else [])
                for k in range(KH):
                    for i, (z, w) in enumerate(passes):
                        last = pe.matmul(TA[:, D:2 * D], z[:, P * k:P * k + P], w[:, k, :],
                                         start=(k == 0 and i == 0), stop=(k == KH - 1 and i == len(passes) - 1))
                last.then_inc(at_y, 1)

            def turn_x(u):
                since(pe, f_xn, u + 1)
                for k in range(KH):
                    last = pe.transpose(TF[:, D + P * k:D + P * k + P], xn[:, P * k:P * k + P], ident)
                last.then_inc(f_T, 1)

            def router(u):
                since(pe, f_hi, u + 1)
                since(pe, f_lo, u + 1)
                for k in range(KH):
                    pe.matmul(TF[:, D:D + 2 * E], x_hi[:, P * k:P * k + P], wr[:, k, :], start=(k == 0), stop=False,
                              skip_group_check=True)
                    last = pe.matmul(TF[:, D:D + E], x_lo[:, P * k:P * k + P], wr[:, k, 0:E], start=False,
                                     stop=(k == KH - 1), skip_group_check=True)
                last.then_inc(f_lg, 1)

            def expert(u, g, m):
                cols = slice(512 * g, 512 * g + 512)
                if m == 0:
                    since(pe, f_gelu, GROUPS * u + g - 1)
                    pe.matmul(EX[:, g % 2, :], pair[:, g, :], be[:], start=True, stop=False)
                else:
                    k, i = (m - 1) // 3, (m - 1) % 3
                    h, w = ((x_hi, we_hi), (x_hi, we_lo), (x_lo, we_hi))[i]
                    last = pe.matmul(EX[:, g % 2, :], h[:, P * k:P * k + P], w[:, k, cols],
                                     start=False, stop=(m == 6))
                    if m == 6:
                        last.then_inc(f_ex, 1)

            def experts(u, g):
                for m in range(7):
                    expert(u, g, m)

            def turn_a(u, last_tile):
                since(pe, f_acc, E * u + E)
                if not last_tile:
                    since(pe, f_g, G_STEPS * (u + 1) + 1)
                for k in range(KH):
                    last = pe.transpose(TF[:, P * k:P * k + P], acc[:, 1, P * k:P * k + P], ident)
                last.then_inc(f_aT, 1)

            def mix_out(u):
                since(pe, f_ahi, u + 1)
                since(pe, f_alo, u + 1)
                for k in range(KH):
                    for i, (h, w) in enumerate(((a_hi, wout_hi), (a_hi, wout_lo), (a_lo, wout_hi))):
                        last = pe.matmul(TF[:, 0:D], h[:, P * k:P * k + P], w[:, k, :],
                                         start=(k == 0 and i == 0), stop=(k == KH - 1 and i == 2))
                last.then_inc(f_y, 1)

            def step(n, kind, last, front, mix, tail):
                if last and not kind:
                    turn_z(n - 1)
                if kind:
                    scores(n, 0, n - 2 if tail else None, last)
                elif tail:
                    experts(n - 2, 2)
                if kind:
                    scores(n, 1, n - 2 if tail else None, last)
                if last and not kind:
                    project_out(last, n - 1)
                if tail and not kind:
                    experts(n - 2, 3)
                if front:
                    turn_h(n + 1)
                if kind:
                    state_products(kind, n)
                if mix:
                    turn_x(n - 1)
                if at(n, NT - 1):
                    pe.wait_ge(s_bhi, 3)
                    pe.wait_ge(s_blo, 3)
                if front:
                    project(front, n + 1, "qk")
                if at(n, 1):
                    pe.wait_ge(s_bhi, 2)
                    pe.wait_ge(s_blo, 2)
                    pe.wait_ge(s_mhi, 1)
                    pe.wait_ge(s_mlo, 1)
                    pe.wait_ge(s_be, 2)
                    pe.wait_ge(s_elo, 2)
                    pe.wait_ge(s_ehi, 2)
                if at(n, 2 * NT - 1):
                    heads(n, 0)
                    heads(n, 1)
                if mix:
                    router(n - 1)
                if at(n, 1):
                    experts(0, 0)
                    heads(1, 0)
                elif kind and not at(n, 2 * NT - 1):
                    heads(n, 0, n - 1 if mix else None)
                elif mix:
                    experts(n - 1, 0)
                if tail:
                    turn_a(n - 2, not mix)
                if front:
                    turn_qk(n + 1)
                if kind and not at(n, 2 * NT - 1):
                    heads(n, 1, n - 1 if mix else None)
                elif mix:
                    experts(n - 1, 1)
                if front:
                    project(front, n + 1, "v")
                if tail:
                    mix_out(n - 2)

            sum_magnitudes(0)
            pe.wait_ge(ld_c, 16)
            turn_h(0)
            project("a", 0, "qk")
            project("a", 0, "v")
            sum_magnitudes(1)
            turn_qk(0)
            pe.wait_ge(ld_fold, 16 * 3)
            for i in range(8):
                fold(0, i)
            steps(pe, step)

        @block.vector
        def _(dve):
            def magnitudes(i, w):
                dve.tensor_reduce(absum[:, i:i + 1], w, AX.X, ALU.add, apply_absolute_value=True).then_inc(s_abs, 1)

            def mean_magnitude(m, count):
                dve.wait_ge(s_sum, m + 1)
                dve.tensor_scalar(wmean[:, m:m + 1], (TA, TF)[m][:, 0:1], 1.0 / count, 1e-5, ALU.mult,
                                  ALU.max).then_inc(s_round, 1)
                dve.wait_ge(s_round, (KH * 2 + 1) * m + 1)
                dve.reciprocal(wscale[:, m:m + 1], wmean[:, m:m + 1]).then_inc(s_mean, 1)
                dve.wait_ge(s_mean, m + 1)

            def ternary(m, src, tmp, dst):
                r0 = (KH * 2 + 1) * m
                for k in range(KH):
                    dve.tensor_scalar(tmp[:, k, :], src[:, k, :], wscale[:, m:m + 1], ROUND, ALU.mult,
                                      ALU.add).then_inc(s_round, 1)
                if m == 0:
                    lo_h(0)
                for k in range(KH):
                    dve.wait_ge(s_round, r0 + 2 + k)
                    dve.tensor_scalar(tmp[:, k, :], tmp[:, k, :], ROUND - 1.0, ROUND + 1.0, ALU.max,
                                      ALU.min).then_inc(s_round, 1)
                for k in range(KH):
                    dve.wait_ge(s_round, r0 + 4 + k)
                    dve.tensor_scalar(dst[:, k, :], tmp[:, k, :], ROUND, None, ALU.subtract).then_inc(s_tern, 1)

            def tile_of(kind, n):
                src, slot = (xs, n) if kind == "a" else (xf, n - NT)
                return src[:, slot, :] if isinstance(slot, int) else src[:, bass.ds(slot, 1), :]

            def prep(kind, n):
                xt = tile_of(kind, n)
                dve.bn_stats(st_a[:], xt).then_inc(at_st, 1)
                since(dve, at_st, n + 1)
                dve.sem_inc(passed, 1)
                dve.bn_aggr(mv_a[:], st_a[:]).then_inc(at_mv, 1)
                since(dve, at_mv, n + 1)
                if kind == "a":
                    dve.tensor_scalar(var_a[:], mv_a[:, 1:2], 1.0 + EPS32, LN_EPS * EPS32, ALU.mult,
                                      ALU.add).then_inc(at_u, 1)
                    since(dve, at_hT, n)
                    dve.scalar_tensor_tensor(out=hn[:], in0=xt, scalar=mv_a[:, 0:1], in1=rw[:, R_QKVN:R_QKVN + D],
                                             op0=ALU.subtract, op1=ALU.mult).then_inc(at_h, 1)
                else:
                    dve.tensor_scalar(var_a[:], mv_a[:, 1:2], LN_EPS, None, ALU.add).then_inc(at_u, 1)
                    since(dve, at_hT, n)
                    dve.tensor_scalar(hn[:], xt, mv_a[:, 0:1], None, ALU.subtract).then_inc(at_h, 1)

            def lo_h(n):
                since(dve, at_hi, n + 1)
                dve.tensor_tensor(h_lo[:], S[:, 0:D], h_hi[:].bitcast(F32), ALU.subtract).then_inc(at_lo, 1)

            def features(n):
                since(dve, at_rs, n + 1)
                since(dve, at_proj, n + 1)
                dve.scalar_tensor_tensor(out=f1[:], in0=S[:, 0:512], scalar=rs_a[:, 0:1], in1=rw[:, R_B1:R_B1 + 512],
                                         op0=ALU.mult, op1=ALU.add)
                dve.scalar_tensor_tensor(out=f2[:], in0=S[:, 512:1024], scalar=rs_a[:, 0:1],
                                         in1=rw[:, R_B2:R_B2 + 512], op0=ALU.mult, op1=ALU.add).then_inc(at_f, 1)
                since(dve, at_f, n - NT + 1)
                dve.tensor_tensor(qk[:, D:2 * D], f1[:, D:2 * D], f2[:, D:2 * D], ALU.mult).then_inc(at_qk, 1)

            def even_odd_k(n):
                since(dve, at_turned, 2 * n + 2)
                dve.tensor_tensor(kT[:].rearrange("p e k t -> p e (k t)"),
                                  S[:, 0:D].unsqueeze(1).to_broadcast([P, 2, D]),
                                  c[:, C_EVEN:C_EVEN + 2].unsqueeze(2).to_broadcast([P, 2, D]),
                                  ALU.mult).then_inc(at_kT, 1)

            def mask(kind, n, half):
                since(dve, at_sc, 2 * n + 1 + half)
                m = (decay[:, 8 * half:8 * half + 8, :] if kind == "a" else
                     causal.unsqueeze(1).to_broadcast([P, 8, P]))
                dve.tensor_tensor(pr[:, 8 * half:8 * half + 8, :],
                                  S[:, 1024 * half:1024 * half + 1024].rearrange("p (s t) -> p s t", t=P), m,
                                  ALU.mult).then_inc(at_p, 1)

            def outputs(kind, n):
                if kind == "a":
                    since(dve, at_ocopy, n + 1)
                    dve.tensor_tensor(z2[:], o_sb[:], norm2[:], ALU.mult).then_inc(at_z2, 1)
                else:
                    since(dve, at_sq, n + 1)
                    dve.tensor_reduce(u2[:], sq[:].rearrange("p (h d) -> p h d", d=DH), AX.X, ALU.add).then_inc(at_u1, 1)
                    since(dve, at_u1, n + 1)
                    dve.tensor_scalar(u2[:], u2[:], 1.0 / DH, HEAD_EPS / QK_SCALE ** 2, ALU.mult,
                                      ALU.add).then_inc(at_u2, 1)

            def output_scales(kind, n):
                if kind == "a":
                    dve.tensor_tensor(z1[:], o_sb[:], rw[:, R_NORM:R_NORM + D], ALU.mult).then_inc(at_z1, 1)
                    since(dve, at_sq, n + 1)
                    dve.tensor_scalar(u1[:], sums[:, 0:1], EPS32 / D, EPS32 * NORM_EPS / QK_SCALE ** 2, ALU.mult,
                                      ALU.add).then_inc(at_u1, 1)
                    since(dve, s_sq2, n + 1)
                    since(dve, at_u1, n + 1)
                    dve.scalar_tensor_tensor(out=u2[:, 0:1], in0=sums[:, 1:2], scalar=1.0 / D, in1=u1[:],
                                             op0=ALU.mult, op1=ALU.add).then_inc(at_u2, 1)
                else:
                    since(dve, at_r2, n + 1)
                    dve.tensor_tensor(z2[:].rearrange("p (h d) -> p h d", d=DH),
                                      TA[:, 0:D].rearrange("p (h d) -> p h d", d=DH),
                                      r2[:].unsqueeze(2).to_broadcast([P, HEADS, DH]), ALU.mult).then_inc(at_z2, 1)

            def add_state(kind, n):
                since(dve, at_sbd, n + 1)
                since(dve, at_kv, n + 1)
                if kind == "a":
                    for f in range(KH):
                        last = dve.scalar_tensor_tensor(
                            out=state_a[:, f, :], in0=state_a[:, f, :], scalar=lam_p[:, f:f + 1],
                            in1=TA[:, D + P * f:D + P * f + P], op0=ALU.mult, op1=ALU.add)
                    last.then_inc(at_state, 1)
                else:
                    dve.tensor_tensor(state_b[:], state_b[:], TA[:, D:2 * D].rearrange("p (f t) -> p f t", f=KH),
                                      ALU.add).then_inc(at_state, 1)

            def lo_z(n):
                since(dve, at_zhi, n + 1)
                dve.tensor_tensor(z_lo[:], TA[:, 0:D], z_hi[:].bitcast(F32), ALU.subtract).then_inc(at_zlo, 1)

            def residual_a(kind, n):
                xt = tile_of(kind, n)
                since(dve, f_xr, n)
                since(dve, at_y, n + 1)
                if kind == "a":
                    since(dve, at_r2, n + 1)
                    dve.scalar_tensor_tensor(out=xc[:], in0=TA[:, D:2 * D], scalar=r2m[:, 0:1], in1=xt,
                                             op0=ALU.mult, op1=ALU.add).then_inc(at_x, 1)
                else:
                    dve.tensor_tensor(xc[:], TA[:, D:2 * D], xt, ALU.add).then_inc(at_x, 1)

            def stats_x(u):
                since(dve, at_x, u + 1)
                dve.bn_stats(st_f[:], xc[:]).then_inc(f_st, 1)
                since(dve, f_st, u + 1)
                dve.sem_inc(passed, 1)
                dve.bn_aggr(mv_f[:], st_f[:]).then_inc(f_mv, 1)
                since(dve, f_mv, u + 1)
                dve.tensor_scalar(var_f[:], mv_f[:, 1:2], LN_EPS, None, ALU.add).then_inc(f_u, 1)

            def norm_x(u):
                since(dve, f_T, u)
                since(dve, f_rs, u + 1)
                dve.tensor_scalar(xn[:], xc[:], mv_f[:, 0:1], rs_f[:, 0:1], ALU.subtract, ALU.mult).then_inc(f_xn, 1)

            def lo_x(u):
                since(dve, f_hi, u + 1)
                dve.tensor_tensor(x_lo[:], TF[:, D:2 * D], x_hi[:].bitcast(F32), ALU.subtract).then_inc(f_lo, 1)

            def choose(u):
                since(dve, f_lg, u + 1)
                dve.tensor_tensor(lg1[:], TF[:, D + E:D + 2 * E], rw[:, R_RB:R_RB + E], ALU.add).then_inc(f_l1, 1)
                since(dve, f_l1, u + 1)
                dve.tensor_tensor(lg[:], TF[:, D:D + E], lg1[:], ALU.add).then_inc(f_g, 1)
                since(dve, f_g, G_STEPS * u + 1)
                dve.sem_inc(passed, 1)
                dve.max(m8[:], lg[:]).then_inc(f_g, 1)
                since(dve, f_g, G_STEPS * u + 2)
                dve.tensor_tensor(dl[:], m8[:, 0:1], m8[:, 1:2], ALU.subtract).then_inc(f_d, 1)
                dve.max_index(ix[:], m8[:], lg[:]).then_inc(f_g, 1)
                since(dve, f_g, G_STEPS * u + 3)
                dve.tensor_copy(ixf[:], ix[:, 0:2]).then_inc(f_g, 1)
                since(dve, f_th, u + 1)
                dve.tensor_scalar(g12[:, 0:1], th[:], 0.5, 0.5, ALU.mult, ALU.add)
                dve.tensor_scalar(g12[:, 1:2], th[:], -0.5, 0.5, ALU.mult, ALU.add).then_inc(f_g, 1)
                since(dve, f_g, G_STEPS * u + 5)
                for i in range(2):
                    dve.tensor_scalar(oh[:, i, :], c[:, C_IOTA:C_IOTA + E], ixf[:, i:i + 1], g12[:, i:i + 1],
                                      ALU.is_equal, ALU.mult).then_inc(f_g, 1)
                since(dve, f_g, G_STEPS * u + 7)
                dve.tensor_tensor(gates[:], oh[:, 0, :], oh[:, 1, :], ALU.add).then_inc(f_g, 1)
                since(dve, f_g, G_STEPS * u + 8)

            def combine(u, g):
                since(dve, f_gelu, GROUPS * u + g + 1)
                for e in (2 * g, 2 * g + 1):
                    h = hb[:, g, D * (e % 2):D * (e % 2) + D]
                    if e == 0:
                        since(dve, f_aT, u)
                        dve.tensor_scalar(acc[:, 0, :], h, gates[:, 0:1], None, ALU.mult).then_inc(f_acc, 1)
                    else:
                        since(dve, f_acc, E * u + e)
                        dve.scalar_tensor_tensor(out=acc[:, e % 2, :], in0=h, scalar=gates[:, e:e + 1],
                                                 in1=acc[:, (e + 1) % 2, :], op0=ALU.mult, op1=ALU.add).then_inc(f_acc, 1)

            def lo_a(u):
                since(dve, f_ahi, u + 1)
                dve.tensor_tensor(a_lo[:], TF[:, 0:D], a_hi[:].bitcast(F32), ALU.subtract).then_inc(f_alo, 1)

            def residual_f(u):
                xt = xf[:, u, :] if isinstance(u, int) else xf[:, bass.ds(u, 1), :]
                since(dve, f_xr, u + 1)
                since(dve, f_y, u + 1)
                dve.tensor_tensor(xt, TF[:, 0:D], xr[:], ALU.add).then_inc(f_x, 1)

            def step(n, kind, last, front, mix, tail):
                if front:
                    prep(front, n + 1)
                if last:
                    lo_z(n - 1)
                if at(n, 0):
                    dve.wait_ge(s_decay0, 1)
                if kind:
                    mask(kind, n, 0)
                if at(n, 0):
                    folded_lo(0)
                if last:
                    residual_a(last, n - 1)
                    stats_x(n - 1)
                if tail:
                    combine(n - 2, 2)
                if last:
                    norm_x(n - 1)
                if front:
                    lo_h(n + 1)
                if kind:
                    add_state(kind, n)
                if mix:
                    lo_x(n - 1)
                if at(n, 0):
                    dve.wait_ge(s_decay1, 1)
                if kind:
                    mask(kind, n, 1)
                if tail:
                    combine(n - 2, 3)
                if front == "b":
                    features(n + 1)
                if at(n, 2 * NT - 1):
                    outputs(kind, n)
                if mix:
                    choose(n - 1)
                    combine(n - 1, 0)
                if tail:
                    lo_a(n - 2)
                if at(n, 0):
                    mixture_lo()
                    dve.wait_ge(s_ehi, 1)
                    dve.tensor_tensor(we_lo[:, 0, :], we_f[:, 0, :], we_hi[:, 0, :].bitcast(F32),
                                      ALU.subtract).then_inc(s_elo, 1)
                if at(n, 1):
                    dve.wait_ge(s_bhi, 3)
                    dve.tensor_tensor(wb_lo[:, :, 4 * D:5 * D], wv_f[:], wb_hi[:, :, 4 * D:5 * D].bitcast(F32),
                                      ALU.subtract)
                    dve.tensor_tensor(wo_lo[:], wo_s[:], wo_hi[:].bitcast(F32), ALU.subtract).then_inc(s_blo, 1)
                if front:
                    even_odd_k(n + 1)
                if kind and not at(n, 2 * NT - 1):
                    outputs(kind, n)
                if kind == "a" or at(n, 2 * NT - 1):
                    output_scales(kind, n)
                if mix:
                    combine(n - 1, 1)
                if tail:
                    residual_f(n - 2)
                if kind == "b" and not at(n, 2 * NT - 1):
                    output_scales(kind, n)
                if at(n, 0):
                    folded_lo(1)
                    dve.wait_ge(ld_rows, 16)

            def folded_lo(k):
                dve.wait_ge(s_bhi, k + 1)
                dve.tensor_tensor(wb_lo[:, k, 0:4 * D], EX[:].rearrange("p g n -> p (g n)"),
                                  wb_hi[:, k, 0:4 * D].bitcast(F32), ALU.subtract).then_inc(s_blo, 1)

            def mixture_lo():
                dve.wait_ge(s_be, 1)
                dve.scalar_tensor_tensor(out=be[0:2 * GROUPS, :], in0=be[0:2 * GROUPS, :].bitcast(F32),
                                         scalar=c[0:2 * GROUPS, C_SECOND:C_SECOND + 1], in1=be_f[:], op0=ALU.mult,
                                         op1=ALU.add).then_inc(s_be, 1)
                dve.wait_ge(s_mhi, 1)
                dve.tensor_tensor(wr[:, :, E:2 * E], sm[:, S_ROUTER:S_ROUTER + KH * E].rearrange("p (k e) -> p k e", k=KH),
                                  wr[:, :, 0:E].bitcast(F32), ALU.subtract)
                dve.tensor_tensor(wout_lo[:], wout_f[:], wout_hi[:].bitcast(F32), ALU.subtract).then_inc(s_mlo, 1)
                dve.wait_ge(ld_b, 16 * 2)
                dve.tensor_scalar(wo_s[:], wo_f[:], sm[:, S_HNORM:S_HNORM + 1], None, ALU.mult).then_inc(s_wos, 1)

            for k in range(KH):
                dve.wait_ge((ld_wqkv0, ld_wqkv1)[k], 16)
                magnitudes(k, wqkv_f[:, k, :])
            dve.wait_ge(ld_sm, 16)
            dve.tensor_scalar(neg_s[:], sm[:, S_S:S_S + HEADS], -1.0, None, ALU.mult).then_inc(s_neg, 1)
            dve.tensor_scalar(neg_sf[:], sm[:, S_DECAY:S_DECAY + KH], -1.0, None, ALU.mult).then_inc(s_neg, 1)
            dve.wait_ge(ld_x0, 16)
            dve.wait_ge(ld_norms, 16)
            prep("a", 0)
            mean_magnitude(0, 3 * D * D)
            ternary(0, wqkv_f, tern, wqkv_t)
            dve.wait_ge(ld_wproj, 16)
            magnitudes(KH, wproj_f[:].rearrange("p k n -> p (k n)"))
            even_odd_k(0)
            dve.wait_ge(s_exp, 2)
            dve.tensor_tensor(decay[:, 0:8, :], decay[:, 0:8, :], causal.unsqueeze(1).to_broadcast([P, 8, P]),
                              ALU.mult).then_inc(s_decay0, 1)
            mean_magnitude(1, D * D)
            ternary(1, wproj_f, tern2, wproj_t)
            dve.wait_ge(s_norm2, 1)
            dve.wait_ge(ld_x, 16)
            steps(dve, step)


def halves(a):
    return np.ascontiguousarray(a.reshape(KH, P, -1).transpose(1, 0, 2))


def constants():
    p, t = np.arange(P)[:, None], np.arange(P)[None, :]
    a = np.zeros((P, C_END), np.float32)
    a[:, C_ID:C_ID + P] = p == t
    a[:, C_CAUSAL:C_CAUSAL + P] = p <= t
    a[:, C_DIFF:C_DIFF + P] = np.maximum(t - p, 0)
    a[:, C_BLOCK:C_BLOCK + P] = p // DH == t // DH
    a[:, C_TT:C_TT + P] = t
    for g in range(GROUPS):
        a[2 * g:2 * g + 2, C_GROUP + g] = 1
    a[:, C_IOTA:C_IOTA + E] = np.arange(E)
    a[:, C_EVEN:C_EVEN + 1] = p // DH % 2 == 0
    a[:, C_ODD:C_ODD + 1] = p // DH % 2 == 1
    a[1:2 * GROUPS:2, C_SECOND] = -1
    a[:, C_REV:C_REV + 1] = P - p
    return a


def kernel(**inputs):
    import concourse.bacc as bacc
    from concourse.bass_utils import run_bass_kernel_spmd

    a = {k: np.asarray(w) for k, w in inputs.items()}
    A, B, F = "L0_attn_a_", "L0_attn_b_", "L0_ffn_"
    small = np.zeros((P, S_END), np.float32)
    small[:, S_DECAY:S_DECAY + KH] = np.repeat(a[A + "s"], DH).reshape(KH, P).T
    small[:, S_HNORM] = np.tile(a[B + "norm_w"], P // DH)
    small[:, S_ROUTER:S_S] = halves(a[F + "router_w"]).reshape(P, KH * E)
    small[:, S_S:S_END] = a[A + "s"]
    rows = np.concatenate([
        a[A + "qkv_norm_w"], a[A + "norm_w"], a[A + "proj_norm_w"],
        np.tile(a[B + "fq1_b"], HEADS), np.tile(a[B + "fk1_b"], HEADS),
        np.tile(a[B + "fq2_b"], HEADS), np.tile(a[B + "fk2_b"], HEADS),
        a[F + "out_b"], a[F + "router_b"]])[None, :]
    bdiag = np.zeros((P, 4, P), np.float32)
    for m, name in enumerate(("fq1_w", "fk1_w", "fq2_w", "fk2_w")):
        for h in range(P // DH):
            bdiag[DH * h:DH * h + DH, m, DH * h:DH * h + DH] = a[B + name].T
    experts = a[F + "expert_w"].transpose(1, 0, 2).reshape(D, E * D)
    arrays = {
        "x": a[A + "x"], "cst": constants(), "small": small, "rows": rows,
        "wqkv": halves(a[A + "qkv_w"].T), "wproj": halves(a[A + "proj_w"].T), "bdiag": bdiag,
        "wq": halves(a[B + "wq"]), "wk": halves(a[B + "wk"]), "wv": halves(a[B + "wv"].T),
        "wo": halves(a[B + "wo"].T), "wexp": halves(experts),
        "bexp": np.repeat(a[F + "expert_b"].reshape(GROUPS, 512), 2, axis=0), "wout": halves(a[F + "out_w"]),
    }
    arrays = {f"in_{k}": np.ascontiguousarray(w) for k, w in arrays.items()}
    nc = bacc.Bacc("TRN2", target_bir_lowering=False, num_devices=1)
    args = [nc.dram_tensor(k, w.shape, mybir.dt.from_np(w.dtype), kind="ExternalInput").ap() for k, w in arrays.items()]
    args.append(nc.dram_tensor("out_0", (1, T, D), F32, kind="ExternalOutput").ap())
    build(nc, *args)
    r = run_bass_kernel_spmd(nc, [arrays], core_ids=[0])
    return r.results[0]["out_0"]
```
